# Optimizing a Trainium2 kernel written in Bass

```python
import numpy as np
import jax
import jax.numpy as jnp

def _softmax(x, axis=-1):
    return jax.nn.softmax(x, axis=axis)

def _gelu(x):
    return jax.nn.gelu(x, approximate=True)

def _silu(x):
    return jax.nn.silu(x)

def _sigmoid(x):
    return jax.nn.sigmoid(x)

def _layernorm(x, axis=-1, eps=1e-05):
    m = jnp.mean(x, axis=axis, keepdims=True)
    v = jnp.var(x, axis=axis, keepdims=True)
    return (x - m) / jnp.sqrt(v + eps)

def _scatter_add(tgt, idx, src, axis=0):
    return tgt.at[idx].add(src)

def _segment_sum(src, seg, n):
    return jax.ops.segment_sum(src, seg, n)
kernel_name = 'mk_adaln_d1_jaxref_r8_96b43c'

def setup_inputs(seed: int=0):
    np.random.seed(seed)
    _w = jnp.asarray

    def _L0_attn_setup():
        import jax, jax.numpy as jnp
        import numpy as np
        L, H, D, DH, DF = (4, 16, 128, 64, 512)
        B, S = (4, 128)

        def layer_norm(x, g, b):
            mu = jnp.mean(x, axis=-1, keepdims=True)
            var = jnp.mean((x - mu) ** 2, axis=-1, keepdims=True)
            return (x - mu) * jax.lax.rsqrt(var + 1e-05) * g + b

        def pos_encoding(seq_len, d):
            pos = jnp.arange(seq_len - 1, -1, -1, dtype=jnp.float32)
            freq = 1.0 / 10000.0 ** (jnp.arange(0, d, 2, dtype=jnp.float32) / d)
            ang = pos[:, None] * freq[None, :]
            return jnp.concatenate([jnp.sin(ang), jnp.cos(ang)], axis=-1)
        key = jax.random.key(seed)
        ks = jax.random.split(key, 16)
        s = 0.02
        return {'x': jax.random.normal(ks[0], (B, S, D), jnp.float32), 'W_qkv': jax.random.normal(ks[1], (L, D, 3 * H * DH), jnp.float32) * s, 'W_r': jax.random.normal(ks[2], (L, D, H * DH), jnp.float32) * s, 'W_o': jax.random.normal(ks[3], (L, H * DH, D), jnp.float32) * s, 'u': jax.random.normal(ks[4], (H, DH), jnp.float32) * s, 'v': jax.random.normal(ks[5], (H, DH), jnp.float32) * s, 'ln1_g': jnp.ones((L, D), jnp.float32), 'ln1_b': jnp.zeros((L, D), jnp.float32), 'W_ff1': jax.random.normal(ks[6], (L, D, DF), jnp.float32) * s, 'b_ff1': jnp.zeros((L, DF), jnp.float32), 'W_ff2': jax.random.normal(ks[7], (L, DF, D), jnp.float32) * s, 'b_ff2': jnp.zeros((L, D), jnp.float32), 'ln2_g': jnp.ones((L, D), jnp.float32), 'ln2_b': jnp.zeros((L, D), jnp.float32)}
    _L0_attn_in = _L0_attn_setup()

    def _L0_ffn_setup():
        import jax, jax.numpy as jnp
        import numpy as np
        B, S, D, E, H, DO = (4, 256, 128, 8, 512, 128)
        TOP_K = 2
        LN_EPS = 1e-05
        key = jax.random.key(seed)
        ks = jax.random.split(key, 9)
        s = 0.02
        return {'x': jax.random.normal(ks[0], (B, S, D), dtype=jnp.float32), 'W1': jax.random.normal(ks[1], (E, D, H), dtype=jnp.float32) * s, 'b1': jnp.zeros((E, H), dtype=jnp.float32), 'W2': jax.random.normal(ks[2], (E, H, DO), dtype=jnp.float32) * s, 'b2': jnp.zeros((E, DO), dtype=jnp.float32), 'gate_W': jax.random.normal(ks[3], (D, E), dtype=jnp.float32) * s, 'shared_W': jax.random.normal(ks[4], (D, DO), dtype=jnp.float32) * s, 'shared_b': jnp.zeros((DO,), dtype=jnp.float32), 'gamma': jnp.ones((DO,), dtype=jnp.float32), 'beta': jnp.zeros((DO,), dtype=jnp.float32)}
    _L0_ffn_in = _L0_ffn_setup()
    _L0_c = _w((lambda *s: np.random.randn(*s).astype(np.float32) * 0.05)(4, 128))
    _L0_wmod = _w((lambda *s: np.random.randn(*s).astype(np.float32) * 0.05)(128, 6 * 128) * 128 ** (-0.5))
    _d = {'L0_attn_x': _L0_attn_in['x'], 'L0_attn_W_qkv': _L0_attn_in['W_qkv'], 'L0_attn_W_r': _L0_attn_in['W_r'], 'L0_attn_W_o': _L0_attn_in['W_o'], 'L0_attn_u': _L0_attn_in['u'], 'L0_attn_v': _L0_attn_in['v'], 'L0_attn_ln1_g': _L0_attn_in['ln1_g'], 'L0_attn_ln1_b': _L0_attn_in['ln1_b'], 'L0_attn_W_ff1': _L0_attn_in['W_ff1'], 'L0_attn_b_ff1': _L0_attn_in['b_ff1'], 'L0_attn_W_ff2': _L0_attn_in['W_ff2'], 'L0_attn_b_ff2': _L0_attn_in['b_ff2'], 'L0_attn_ln2_g': _L0_attn_in['ln2_g'], 'L0_attn_ln2_b': _L0_attn_in['ln2_b'], 'L0_ffn_W1': _L0_ffn_in['W1'], 'L0_ffn_b1': _L0_ffn_in['b1'], 'L0_ffn_W2': _L0_ffn_in['W2'], 'L0_ffn_b2': _L0_ffn_in['b2'], 'L0_ffn_gate_W': _L0_ffn_in['gate_W'], 'L0_ffn_shared_W': _L0_ffn_in['shared_W'], 'L0_ffn_shared_b': _L0_ffn_in['shared_b'], 'L0_ffn_gamma': _L0_ffn_in['gamma'], 'L0_ffn_beta': _L0_ffn_in['beta'], 'L0_c': _L0_c, 'L0_wmod': _L0_wmod}
    _x0 = _d['L0_attn_x']
    _d['L0_attn_x'] = jax.random.normal(jax.random.fold_in(jax.random.key(seed), 1), (4, 512, 128), dtype=_x0.dtype)
    del _x0
    return _d

def reference(L0_attn_x, L0_attn_W_qkv, L0_attn_W_r, L0_attn_W_o, L0_attn_u, L0_attn_v, L0_attn_ln1_g, L0_attn_ln1_b, L0_attn_W_ff1, L0_attn_b_ff1, L0_attn_W_ff2, L0_attn_b_ff2, L0_attn_ln2_g, L0_attn_ln2_b, L0_ffn_W1, L0_ffn_b1, L0_ffn_W2, L0_ffn_b2, L0_ffn_gate_W, L0_ffn_shared_W, L0_ffn_shared_b, L0_ffn_gamma, L0_ffn_beta, L0_c, L0_wmod):

    def _L0_attn_ref(x, W_qkv, W_r, W_o, u, v, ln1_g, ln1_b, W_ff1, b_ff1, W_ff2, b_ff2, ln2_g, ln2_b):
        import jax, jax.numpy as jnp
        import numpy as np
        L, H, D, DH, DF = (4, 16, 128, 64, 512)
        B, S = (4, 128)

        def layer_norm(x, g, b):
            mu = jnp.mean(x, axis=-1, keepdims=True)
            var = jnp.mean((x - mu) ** 2, axis=-1, keepdims=True)
            return (x - mu) * jax.lax.rsqrt(var + 1e-05) * g + b

        def pos_encoding(seq_len, d):
            pos = jnp.arange(seq_len - 1, -1, -1, dtype=jnp.float32)
            freq = 1.0 / 10000.0 ** (jnp.arange(0, d, 2, dtype=jnp.float32) / d)
            ang = pos[:, None] * freq[None, :]
            return jnp.concatenate([jnp.sin(ang), jnp.cos(ang)], axis=-1)
        b, s_len, _ = x.shape
        r = pos_encoding(s_len, D)
        h = x
        inv_sqrt_d = 1.0 / jnp.sqrt(jnp.float32(DH))
        for i in range(L):
            qkv = h @ W_qkv[i]
            q, k, val = jnp.split(qkv, 3, axis=-1)
            q = q.reshape(b, s_len, H, DH)
            k = k.reshape(b, s_len, H, DH)
            val = val.reshape(b, s_len, H, DH)
            kr = (r @ W_r[i]).reshape(s_len, H, DH)
            AC = jnp.einsum('bqhd,bkhd->bhqk', q + u, k)
            BD = jnp.einsum('bqhd,khd->bhqk', q + v, kr)
            prob = jax.nn.softmax((AC + BD) * inv_sqrt_d, axis=-1)
            vec = jnp.einsum('bhqk,bkhd->bqhd', prob, val).reshape(b, s_len, H * DH)
            h = layer_norm(h + vec @ W_o[i], ln1_g[i], ln1_b[i])
            ff = jax.nn.relu(h @ W_ff1[i] + b_ff1[i]) @ W_ff2[i] + b_ff2[i]
            h = layer_norm(ff, ln2_g[i], ln2_b[i])
        return h

    def _L0_ffn_ref(x, W1, b1, W2, b2, gate_W, shared_W, shared_b, gamma, beta):
        import jax, jax.numpy as jnp
        import numpy as np
        B, S, D, E, H, DO = (4, 256, 128, 8, 512, 128)
        TOP_K = 2
        LN_EPS = 1e-05
        d = x.shape[-1]
        flat = x.reshape(-1, d)
        n_exp = gate_W.shape[-1]
        probs = jax.nn.softmax(flat @ gate_W, axis=-1)
        topk_w, topk_idx = jax.lax.top_k(probs, TOP_K)
        topk_w = topk_w / topk_w.sum(axis=-1, keepdims=True)
        combine = (jax.nn.one_hot(topk_idx, n_exp, dtype=flat.dtype) * topk_w[..., None]).sum(axis=1)
        out = 0.5 * jax.nn.gelu(flat @ shared_W + shared_b, approximate=False)
        for e in range(n_exp):
            h = jax.nn.gelu(flat @ W1[e] + b1[e], approximate=False)
            out = out + combine[:, e:e + 1] * (h @ W2[e] + b2[e])
        mean = out.mean(axis=-1, keepdims=True)
        var = ((out - mean) ** 2).mean(axis=-1, keepdims=True)
        out = (out - mean) * jax.lax.rsqrt(var + LN_EPS) * gamma + beta
        return out.reshape(*x.shape[:-1], out.shape[-1])
    x = L0_attn_x
    mod = (_silu(L0_c) @ L0_wmod).reshape(L0_c.shape[0], 6, 1, -1)
    sa, ca, ga, sb, cb, gb = (mod[:, 0], mod[:, 1], mod[:, 2], mod[:, 3], mod[:, 4], mod[:, 5])
    ga = (2 * (ga >= 0) - 1) * jnp.maximum(jnp.abs(ga), 0.25)
    gb = (2 * (gb >= 0) - 1) * jnp.maximum(jnp.abs(gb), 0.25)
    h = _layernorm(x, axis=-1) * (1 + ca) + sa
    x = x + ga * _L0_attn_ref(h, L0_attn_W_qkv, L0_attn_W_r, L0_attn_W_o, L0_attn_u, L0_attn_v, L0_attn_ln1_g, L0_attn_ln1_b, L0_attn_W_ff1, L0_attn_b_ff1, L0_attn_W_ff2, L0_attn_b_ff2, L0_attn_ln2_g, L0_attn_ln2_b)
    h = _layernorm(x, axis=-1) * (1 + cb) + sb
    x = x + gb * _L0_ffn_ref(h, L0_ffn_W1, L0_ffn_b1, L0_ffn_W2, L0_ffn_b2, L0_ffn_gate_W, L0_ffn_shared_W, L0_ffn_shared_b, L0_ffn_gamma, L0_ffn_beta)
    return x

_drawn_inputs = setup_inputs


def setup_inputs(seed=0):
    import zlib

    import numpy as np

    out = dict(_drawn_inputs(seed))
    spreads = {'L0_attn_ln1_g': (1.0, 0.2),
     'L0_attn_ln1_b': (0.0, 0.1),
     'L0_attn_b_ff1': (0.0, 0.1),
     'L0_attn_b_ff2': (0.0, 0.1),
     'L0_attn_ln2_g': (1.0, 0.2),
     'L0_attn_ln2_b': (0.0, 0.1),
     'L0_ffn_b1': (0.0, 0.1),
     'L0_ffn_b2': (0.0, 0.1),
     'L0_ffn_shared_b': (0.0, 0.1),
     'L0_ffn_gamma': (1.0, 0.2),
     'L0_ffn_beta': (0.0, 0.321)}
    factors = {'L0_attn_W_r': 8.0, 'L0_attn_u': 8.0, 'L0_attn_v': 8.0}
    for name, (base, spread) in spreads.items():
        noise = np.random.default_rng([zlib.crc32(name.encode()), seed]).standard_normal(out[name].shape)
        drawn = base * np.exp(spread * noise) if base else spread * noise
        out[name] = jnp.asarray(drawn.astype(out[name].dtype))
    for name, factor in factors.items():
        out[name] = (out[name] * factor).astype(out[name].dtype)
    return out
```

```python
import concourse.bass as bass
from concourse import mybir
from contextlib import ExitStack

F32 = mybir.dt.float32
F32R = mybir.dt.float32r
ALU = mybir.AluOpType
ACT = mybir.ActivationFunctionType
AX = mybir.AxisListType

P = 128
B = 4
S = 512
D = 128
T = S // P
L = 4
H = 16
DH = 64
HP = H // 2
DF = 512
FB = DF // P
E = 8
NT = HP * 2 * T
EPS = 1e-5
SCALE = DH ** -0.5
N_MOD = 6
SA, CA, GA, SB_, CB, GB = range(N_MOD)


class Turns:

    def __init__(self, eng, sem, start=1, step=1):
        self.eng, self.sem, self.by = eng, sem, step
        self.count = eng.alloc_register(f"turn_{sem.name}")
        eng.reg_mov(self.count, start)

    def wait(self):
        self.eng.wait_ge(self.sem, self.count)
        self.eng.reg_add(self.count, self.count, self.by)


class Counted:

    def __init__(self, eng, sem, step):
        self.eng, self.sem, self.by, self.n = eng, sem, step, 0

    def wait(self):
        self.n += self.by
        self.eng.wait_ge(self.sem, self.n)


class Chain:

    def __init__(self, eng, sem, base=0):
        self.eng, self.sem, self.base, self.n = eng, sem, base, 0

    def step(self, ins):
        self.n += 1
        ins.then_inc(self.sem, 1)

    def wait(self):
        self.eng.wait_ge(self.sem, self.base + self.n)

    def link(self, ins):
        self.step(ins)
        self.wait()


def layer_norm_rows(dve, chain, stats, src, small, count, dst):
    n, (stat, mv, rstd, _, s_stat, s_var, s_rstd) = T, small
    for t in range(n):
        dve.bn_stats(stat[:, t, :], src[:, t, :]).then_inc(s_stat, 1)
    stats.wait()
    for t in range(n):
        chain.step(dve.bn_aggr(mv[:, t, :], stat[:, t, :]))
    chain.wait()
    dve.tensor_scalar(rstd[:], mv[:, :, 1], EPS, None, ALU.add).then_inc(s_var, 1)
    dve.wait_ge(s_rstd, count)
    for t in range(n):
        chain.step(dve.tensor_scalar(dst[:, t, :], src[:, t, :], mv[:, t, 0:1], rstd[:, t:t + 1],
                                     ALU.subtract, ALU.mult))
    chain.wait()


LN_STEPS = 2 * T


def inverse_root(pool, small, count):
    _, _, rstd, exponent, _, s_var, s_rstd = small
    pool.wait_ge(s_var, count)
    pool.tensor_tensor(rstd[:], rstd[:], exponent[:], ALU.pow).then_inc(s_rstd, 1)


def over_tiles(row, n):
    return row.unsqueeze(1).to_broadcast([P, n, D])


def build(nc, x, w_qkv, w_r, w_o, u, v, ln1_g, ln1_b, w_ff1, b_ff1, w_ff2, b_ff2, ln2_g, ln2_b,
          w1, b1, w2, b2, gate_w, shared_w, shared_b, gamma, beta, c, wmod, pos_t, out):
    ctx = ExitStack()
    with ctx:
        ctx.enter_context(nc.allow_non_contiguous_dma(reason="small transposed loads of vectors"))

        def sem(name):
            return ctx.enter_context(nc.semaphore(name))

        def sb_in(stack, name, shape, dt=F32):
            return stack.enter_context(nc.sbuf_tensor(name, shape, dt))

        def sb(name, shape, dt=F32):
            return sb_in(ctx, name, shape, dt)

        bank = [ctx.enter_context(nc.psum_tensor(f"bank{i}", [P, 512], F32)) for i in range(8)]

        ident = sb("ident", [P, P])
        h_tok = sb("h_tok", [P, B * T, D])
        h_feat = sb("h_feat", [P, B, S])
        silu_c = sb("silu_c", [P, B])
        stat = sb("stat", [P, T, 6])
        mv = sb("mv", [P, T, 2])
        rstd = sb("rstd", [P, T])
        exponent = sb("exponent", [P, T])
        small = [(stat, mv, rstd, exponent, sem(f"stat{i}"), sem(f"var{i}"), sem(f"rstd{i}")) for i in range(3)]

        modulate_in(nc, ctx, sem, sb_in, bank, ident, h_tok, h_feat, silu_c, small[0],
                    x, c, wmod)
        transformer(nc, ctx, sem, sb_in, bank, ident, h_tok, h_feat, small[1],
                    w_qkv, w_r, w_o, u, v, ln1_g, ln1_b, w_ff1, b_ff1, w_ff2, b_ff2, ln2_g, ln2_b,
                    pos_t)
        experts(nc, ctx, sem, sb_in, bank, ident, h_tok, silu_c, small[2],
                x, wmod, w1, b1, w2, b2, gate_w, shared_w, shared_b, gamma, beta, out)


def modulate_in(nc, ctx, sem, sb_in, bank, ident, h_tok, h_feat, silu_c, small, x, c, wmod):
    with ExitStack() as own:
        c_feat = sb_in(own, "c_feat", [P, B])
        wm = sb_in(own, "wm_in", [P, 2 * D])
        x_in = sb_in(own, "x_in", [P, B * T, D])
        mod = sb_in(own, "mod_in", [P, B, 2 * D])
        s_id, s_x, s_c, s_wm = sem("in_ident"), sem("in_x"), sem("in_c"), sem("in_wm")
        s_exp, s_silu, s_mod, s_modc = sem("in_exp"), sem("in_silu"), sem("in_mod"), sem("in_modc")
        s_chain, s_h, s_tr, s_tc = sem("in_chain"), sem("in_h"), sem("in_tr"), sem("in_tc")

        with nc.Block() as block:
            @block.sync
            def _(sp):
                sp.dma_start(c_feat[:], c.rearrange("b d -> d b")).then_inc(s_c, 16)
                sp.dma_start(wm[:], wmod[:, 0:2 * D]).then_inc(s_wm, 16)
                sp.dma_start(x_in[:], x.rearrange("b (t p) d -> p (b t) d", p=P)).then_inc(s_x, 16)

            @block.gpsimd
            def _(pool):
                pool.memset(ident[:], 0.0).then_inc(s_id, 1)
                pool.wait_ge(s_id, 1)
                pool.affine_select(out=ident[:], in_=ident[:], compare_op=ALU.not_equal, fill=1.0,
                                   base=0, pattern=[[-1, P]], channel_multiplier=1).then_inc(s_id, 1)
                pool.memset(small[3][:], -0.5).then_inc(s_id, 1)
                pool.wait_ge(s_id, 3)
                for b in range(B):
                    inverse_root(pool, small, b + 1)

            @block.scalar
            def _(act):
                act.wait_ge(s_c, 16)
                act.activation(silu_c[:], c_feat[:], ACT.Exp, scale=-1.0).then_inc(s_exp, 1)
                for b in range(B):
                    act.wait_ge(s_mod, b + 1)
                    act.activation(mod[:, b, :], bank[b][:, 0:2 * D], ACT.Copy).then_inc(s_modc, 1)
                for b in range(B):
                    act.wait_ge(s_tr, b + 1)
                    act.activation(h_feat[:, b, :], bank[4 + b][:], ACT.Copy).then_inc(s_tc, 1)

            @block.vector
            def _(dve):
                ch, stats = Chain(dve, s_chain), Counted(dve, small[4], T)
                dve.wait_ge(s_exp, 1)
                ch.link(dve.tensor_scalar(silu_c[:], silu_c[:], 1.0, None, ALU.add))
                ch.link(dve.reciprocal(silu_c[:], silu_c[:]))
                dve.tensor_tensor(silu_c[:], silu_c[:], c_feat[:], ALU.mult).then_inc(s_silu, 1)
                dve.wait_ge(s_x, 16)
                for b in range(B):
                    rows = h_tok[:, b * T:(b + 1) * T, :]
                    layer_norm_rows(dve, ch, stats, x_in[:, b * T:(b + 1) * T, :], small, b + 1, rows)
                    dve.wait_ge(s_modc, b + 1)
                    ch.link(dve.tensor_scalar(mod[:, b, D:2 * D], mod[:, b, D:2 * D], 1.0, None, ALU.add))
                    ch.link(dve.tensor_tensor(rows, rows, over_tiles(mod[:, b, D:2 * D], T), ALU.mult))
                    dve.tensor_tensor(rows, rows, over_tiles(mod[:, b, 0:D], T), ALU.add)\
                       .then_inc(s_h, 1)

            @block.tensor
            def _(pe):
                pe.wait_ge(s_silu, 1)
                pe.wait_ge(s_wm, 16)
                for b in range(B):
                    pe.matmul(bank[b][:, 0:2 * D], silu_c[:, b:b + 1].to_broadcast([P, P]), wm[:],
                              start=True, stop=True).then_inc(s_mod, 1)
                pe.wait_ge(s_id, 2)
                for b in range(B):
                    pe.wait_ge(s_h, b + 1)
                    for t in range(T):
                        mm = pe.transpose(bank[4 + b][:, t * P:(t + 1) * P], h_tok[:, b * T + t, :],
                                          ident[:])
                    mm.then_inc(s_tr, 1)


def transformer(nc, ctx, sem, sb_in, bank, ident, h_tok, h_feat, small,
                w_qkv, w_r, w_o, u, v, ln1_g, ln1_b, w_ff1, b_ff1, w_ff2, b_ff2, ln2_g, ln2_b, pos_t):
    with ExitStack() as own:
        def sb(name, shape, dt=F32):
            return sb_in(own, name, shape, dt)

        qk_raw = sb("qk_raw", [P, 2 * H * DH])
        qk_hi = sb("qk_hi", [P, 2 * H * DH], F32R)
        qk_lo = sb("qk_lo", [P, 2 * H * DH], F32R)
        r_raw = sb("r_raw", [P, H * DH])
        v_w = sb("v_w", [P, H * DH])
        o_w = sb("o_w", [P, HP, D])
        f1_raw = sb("f1_raw", [P, DF])
        f1_hi = sb("f1_hi", [P, DF], F32R)
        f1_lo = sb("f1_lo", [P, DF], F32R)
        f2_w = sb("f2_w", [P, FB, D])
        rows = sb("rows", [P, 5, D])
        f1_b = sb("f1_b", [P, FB])
        pos = sb("pos", [P, S])
        u_col = sb("u_col", [P, HP])
        v_col = sb("v_col", [P, HP])
        vu_pad = sb("vu_pad", [P, H])
        kr_feat = sb("kr_feat", [P, HP, S])
        kr_bias = sb("kr_bias", [P, H, S])
        x_feat = sb("x_feat", [P, S])
        x_hi = sb("x_hi", [P, S], F32R)
        x_lo = sb("x_lo", [P, S], F32R)
        q_hi = sb("q_hi", [P, 2, 2, S], F32R)
        q_lo = sb("q_lo", [P, 2, 2, S], F32R)
        k_sum = sb("k_sum", [P, S])
        k_hi = sb("k_hi", [P, 2, S], F32R)
        k_lo = sb("k_lo", [P, 2, S], F32R)
        v_tok = sb("v_tok", [P, 2, T, P])
        neg_max = sb("neg_max", [P, 4])
        sums = sb("sums", [P, 2, 2 * T])
        rec = sb("rec", [P, 2 * T])
        prob = sb("prob", [P, 2, S])
        prob_t = sb("prob_t", [P, 2, 2, T, S])
        rec_row = sb("rec_row", [P, S])
        attn = sb("attn", [P, HP, S])
        y = sb("y", [P, T, D])
        ff = prob_t[:, 0, 0, :, :]

        (psS0, psS1, psS2, psT0, psT1, psV, psA, psB) = bank
        psS, psT = (psS0, psS1, psS2), (psT0, psT1)

        s_const, s_raw, s_w, s_uv, s_zero = sem("const"), sem("raw_in"), sem("w_in"), sem("uv"), sem("zero")
        s_split_hi, s_split = sem("split_hi"), sem("split")
        s_kr, s_krc, s_bias, s_biasc = sem("kr"), sem("krc"), sem("bias"), sem("biasc")
        s_xhi, s_x = sem("x_hi"), sem("x_lo")
        s_q, s_qhi, s_qlo = sem("q"), sem("q_hi"), sem("q_lo")
        s_k, s_ksum, s_khi, s_klo = sem("k"), sem("k_sum"), sem("k_hi"), sem("k_lo")
        s_v, s_vc = sem("v"), sem("vc")
        s_S, s_max, s_exp = sem("scores"), sem("max"), sem("exp")
        s_T, s_ca, s_cv = sem("probT"), sem("copied_act"), sem("copied_dve")
        s_pv, s_rec, s_r, s_rc, s_attn = sem("pv"), sem("rec"), sem("r"), sem("rc"), sem("attn")
        s_o, s_z, s_zt, s_zhi, s_zlo = sem("o"), sem("z"), sem("zt"), sem("zhi"), sem("zlo")
        s_f1, s_f1c, s_f2, s_hn, s_ht, s_done = (sem("f1"), sem("f1c"), sem("f2"), sem("hn"),
                                                 sem("ht"), sem("done"))
        s_res = sem("res")
        s_ch = sem("dve_chain")
        CH = 2 * (LN_STEPS + 2)
        N_RAW, N_W = 3, 9

        def three_pass(pe, ps, w_hi, w_lo, m_hi, m_lo):
            pe.matmul(ps, w_hi, m_hi, start=True, stop=False)
            pe.matmul(ps, w_hi, m_lo, start=False, stop=False)
            return pe.matmul(ps, w_lo, m_hi, start=False, stop=True)

        with nc.Block() as block:
            @block.sync
            def _(sp):
                sp.dma_start(pos[:], pos_t).then_inc(s_const, 16)
                sp.dma_start(u_col[:], u.rearrange("(p two) d -> (two d) p", two=2)).then_inc(s_const, 16)
                sp.dma_start(v_col[:], v.rearrange("(p two) d -> (two d) p", two=2)).then_inc(s_const, 16)
                with sp.Fori(0, L) as l:
                    sp.wait_ge(s_biasc, l * H + 1)
                    sp.dma_start(qk_raw[:], w_qkv[l, :, 0:2 * H * DH]).then_inc(s_raw, 16)
                    sp.dma_start(r_raw[:], w_r[l]).then_inc(s_raw, 16)
                    sp.dma_start(f1_raw[:], w_ff1[l]).then_inc(s_raw, 16)
                    sp.wait_ge(s_done, l * B + 1)
                    sp.dma_start(v_w[:], w_qkv[l, :, 2 * H * DH:]).then_inc(s_w, 16)
                    sp.dma_start(o_w[:], w_o[l].rearrange("(p k) n -> k p n", k=P)).then_inc(s_w, 16)
                    sp.dma_start(f2_w[:], w_ff2[l].rearrange("(f k) n -> k f n", k=P)).then_inc(s_w, 16)
                    sp.dma_start(f1_b[:], b_ff1[l].rearrange("(f k) -> k f", k=P)).then_inc(s_w, 16)
                    for i, vec in enumerate((ln1_g, ln1_b, ln2_g, ln2_b, b_ff2)):
                        sp.dma_start(rows[:, i, :], vec[l].unsqueeze(0).to_broadcast([P, D]))\
                          .then_inc(s_w, 16)

            @block.gpsimd
            def _(pool):
                pool.memset(vu_pad[:], 0.0).then_inc(s_zero, 1)
                for t in (q_hi, q_lo):
                    pool.memset(t[:].bitcast(F32), 0.0).then_inc(s_zero, 1)
                with pool.Fori(0, L) as l, pool.Fori(0, B) as b:
                    it = l * B + b
                    for p in range(HP):
                        pool.wait_ge(s_khi, it * HP + p + 1)
                        pool.tensor_tensor(k_lo[:, p % 2, :], k_sum[:], k_hi[:, p % 2, :].bitcast(F32),
                                           ALU.subtract).then_inc(s_klo, 1)
                    inverse_root(pool, small, it * 2 + 1)
                    inverse_root(pool, small, it * 2 + 2)
                    pool.wait_ge(s_hn, it + 1)
                    pool.tensor_copy(h_tok[:, bass.ts(b, T), :], y[:]).then_inc(s_res, 1)

            @block.scalar
            def _(act):
                done_turns, ht_turns = Turns(act, s_done), Turns(act, s_ht)
                act.sem_inc(s_done, 1)
                with act.Fori(0, L) as l:
                    act.wait_ge(s_raw, (l + 1) * 16 * N_RAW)
                    act.activation(qk_hi[:], qk_raw[:], ACT.Copy).then_inc(s_split_hi, 1)
                    act.activation(f1_hi[:], f1_raw[:], ACT.Copy).then_inc(s_split_hi, 1)
                    for p in range(HP):
                        act.wait_ge(s_kr, l * HP + p + 1)
                        act.activation(kr_feat[:, p, :], psS[p % 2][:], ACT.Copy).then_inc(s_krc, 1)
                    with act.Fori(0, B) as b:
                        it = l * B + b
                        done_turns.wait()
                        act.activation(x_hi[:], h_feat[:, b, :], ACT.Copy).then_inc(s_xhi, 1)

                        def q_high(p):
                            act.wait_ge(s_q, it * HP + p + 1)
                            for a in range(2):
                                r = slice(DH * a, DH * a + DH)
                                act.activation(q_hi[r, p % 2, a, :], psA[r, :], ACT.Identity,
                                               bias=u_col[r, p:p + 1]).then_inc(s_qhi, 1)

                        def v_out(p):
                            act.wait_ge(s_v, it * HP + p + 1)
                            act.activation(v_tok[:, p % 2].rearrange("p c n -> p (c n)"), psA[:], ACT.Copy)\
                               .then_inc(s_vc, 1)

                        def r_out(p):
                            act.wait_ge(s_r, it * HP + p + 1)
                            if p >= 1:
                                act.wait_ge(s_attn, it * HP + p)
                            act.activation(rec_row[:], psB[:], ACT.Copy).then_inc(s_rc, 1)

                        q_high(0)
                        v_out(0)
                        for j in range(NT):
                            p, a, t = j // 8, j % 8 // T, j % T
                            act.wait_ge(s_max, it * NT + j + 1)
                            if j >= 2:
                                act.wait_ge(s_T, it * NT + j - 1)
                            act.activation(prob[:, j % 2, :], psS[j % 3][:], ACT.Exp, scale=-1.0,
                                           bias=neg_max[:, j % 4:j % 4 + 1],
                                           accum_out=sums[:, p % 2, j % 8:j % 8 + 1]).then_inc(s_exp, 1)
                            if j % 2 == 1:
                                i = j - 1
                                act.wait_ge(s_T, it * NT + i + 1)
                                act.activation(prob_t[:, p % 2, a, :, (i % T) * P:(i % T + 1) * P],
                                               psT[0].rearrange("p (c q) -> p c q", c=T), ACT.Copy)\
                                   .then_inc(s_ca, 1)
                            if j % 8 == 1 and p + 1 < HP:
                                q_high(p + 1)
                            if j % 8 == 4 and p + 1 < HP:
                                v_out(p + 1)
                            if j % 8 == 5 and p >= 1:
                                r_out(p - 1)
                        r_out(HP - 1)
                        act.wait_ge(s_zt, it + 1)
                        act.activation(x_hi[:], psS1[:], ACT.Copy).then_inc(s_zhi, 1)
                        for f in range(FB):
                            act.wait_ge(s_f1, it * FB + f + 1)
                            act.activation(ff[:, f, :], (psA, psB, psT0, psT1)[f][:], ACT.Relu,
                                           bias=f1_b[:, f:f + 1]).then_inc(s_f1c, 1)
                        ht_turns.wait()
                        act.activation(h_feat[:, b, :], psS2[:], ACT.Copy).then_inc(s_done, 1)

            @block.vector
            def _(dve):
                score_turns, stats = Turns(dve, s_S), Turns(dve, small[4], T, T)
                dve.wait_ge(s_const, 48)
                dve.wait_ge(s_zero, 1)
                for a in range(2):
                    r = slice(DH * a, DH * a + DH)
                    dve.tensor_tensor(vu_pad[r, a::2], v_col[r, :], u_col[r, :], ALU.subtract)\
                       .then_inc(s_uv, 1)
                dve.sem_inc(s_biasc, 1)
                with dve.Fori(0, L) as l:
                    dve.wait_ge(s_split_hi, (l + 1) * 2)
                    dve.tensor_tensor(qk_lo[:], qk_raw[:], qk_hi[:].bitcast(F32), ALU.subtract)\
                       .then_inc(s_split, 1)
                    dve.tensor_tensor(f1_lo[:], f1_raw[:], f1_hi[:].bitcast(F32), ALU.subtract)\
                       .then_inc(s_split, 1)
                    for h in range(H):
                        dve.wait_ge(s_bias, l * H + h + 1)
                        dve.tensor_copy(kr_bias[:, h, :], (psS2, psT0)[h % 2][:]).then_inc(s_biasc, 1)
                    with dve.Fori(0, B) as b:
                        it = l * B + b
                        ch = Chain(dve, s_ch, it * CH)
                        dve.wait_ge(s_xhi, it + 1)
                        dve.tensor_copy(x_feat[:], h_feat[:, b, :]).then_inc(s_x, 1)
                        dve.tensor_tensor(x_lo[:], h_feat[:, b, :], x_hi[:].bitcast(F32), ALU.subtract)\
                           .then_inc(s_x, 1)

                        def k_split(p):
                            dve.wait_ge(s_k, it * HP + p + 1)
                            if p >= 1:
                                dve.wait_ge(s_klo, it * HP + p)
                            dve.tensor_tensor(k_sum[:], psB[:], kr_feat[:, p, :], ALU.add)\
                               .then_inc(s_ksum, 1)
                            dve.wait_ge(s_ksum, it * HP + p + 1)
                            dve.tensor_copy(k_hi[:, p % 2, :], k_sum[:]).then_inc(s_khi, 1)

                        def q_low(p):
                            dve.wait_ge(s_qhi, it * 2 * HP + 2 * p + 2)
                            for a in range(2):
                                r = slice(DH * a, DH * a + DH)
                                dve.scalar_tensor_tensor(out=q_lo[r, p % 2, a, :], in0=psA[r, :],
                                                         scalar=u_col[r, p:p + 1],
                                                         in1=q_hi[r, p % 2, a, :].bitcast(F32),
                                                         op0=ALU.add, op1=ALU.subtract).then_inc(s_qlo, 1)

                        def reciprocals(p):
                            dve.wait_ge(s_exp, it * NT + 8 * p + 8)
                            if p >= 1:
                                dve.wait_ge(s_r, it * HP + p)
                            dve.reciprocal(rec[:], sums[:, p % 2, :]).then_inc(s_rec, 1)

                        def normalise(p):
                            dve.wait_ge(s_rc, it * HP + p + 1)
                            dve.tensor_tensor(attn[:, p, :], psV[:], rec_row[:], ALU.mult)\
                               .then_inc(s_attn, 1)

                        q_low(0)
                        k_split(0)
                        for j in range(NT):
                            p, a, t = j // 8, j % 8 // T, j % T
                            score_turns.wait()
                            dve.tensor_tensor_reduce(psS[j % 3][:], psS[j % 3][:],
                                                     kr_bias[:, 2 * p + a, :], -SCALE, 3e38,
                                                     ALU.add, ALU.min, neg_max[:, j % 4:j % 4 + 1])\
                               .then_inc(s_max, 1)
                            if j % 8 == 1 and p >= 1:
                                reciprocals(p - 1)
                            if j % 8 == 2 and p + 1 < HP:
                                q_low(p + 1)
                            if j % 8 == 3 and p + 1 < HP:
                                k_split(p + 1)
                            if j % 2 == 0 and j >= 2:
                                copy_odd(dve, it, j - 1, prob_t, psT, s_T, s_cv)
                            if j % 8 == 6 and p >= 1:
                                normalise(p - 1)
                        copy_odd(dve, it, NT - 1, prob_t, psT, s_T, s_cv)
                        reciprocals(HP - 1)
                        normalise(HP - 1)
                        dve.wait_ge(s_o, it + 1)
                        ch.link(dve.tensor_tensor(y[:], psS0[:].rearrange("p (t d) -> p t d", t=T),
                                                  h_tok[:, bass.ts(b, T), :], ALU.add))
                        layer_norm_rows(dve, ch, stats, y, small, it * 2 + 1, y)
                        ch.link(dve.tensor_tensor(y[:], y[:], over_tiles(rows[:, 0, :], T), ALU.mult))
                        dve.tensor_tensor(y[:], y[:], over_tiles(rows[:, 1, :], T), ALU.add).then_inc(s_z, 1)
                        dve.wait_ge(s_zhi, it + 1)
                        dve.tensor_tensor(x_lo[:], psS1[:], x_hi[:].bitcast(F32), ALU.subtract)\
                           .then_inc(s_zlo, 1)
                        dve.wait_ge(s_f2, it + 1)
                        ch.link(dve.tensor_tensor(y[:], psV[:].rearrange("p (t d) -> p t d", t=T),
                                                  over_tiles(rows[:, 4, :], T), ALU.add))
                        layer_norm_rows(dve, ch, stats, y, small, it * 2 + 2, y)
                        ch.link(dve.tensor_tensor(y[:], y[:], over_tiles(rows[:, 2, :], T), ALU.mult))
                        dve.tensor_tensor(y[:], y[:], over_tiles(rows[:, 3, :], T), ALU.add).then_inc(s_hn, 1)
                        dve.wait_ge(s_res, it + 1)
                        dve.wait_ge(s_done, it + 2)
                        assert ch.n == CH, ch.n

            @block.tensor
            def _(pe):
                weight_turns = Turns(pe, s_w, 16 * N_W, 16 * N_W)
                pe.wait_ge(s_const, 48)
                pe.wait_ge(s_uv, 2)
                pe.wait_ge(s_zero, 3)
                with pe.Fori(0, L) as l:
                    pe.wait_ge(s_raw, (l + 1) * 16 * N_RAW)
                    for p in range(HP):
                        if p >= 2:
                            pe.wait_ge(s_krc, l * HP + p - 1)
                        pe.matmul(psS[p % 2][:], r_raw[:, p * P:(p + 1) * P], pos[:], start=True,
                                  stop=True).then_inc(s_kr, 1)
                    for h in range(H):
                        pe.wait_ge(s_krc, l * HP + h // 2 + 1)
                        if h >= 2:
                            pe.wait_ge(s_biasc, l * H + h)
                        pe.matmul((psS2, psT0)[h % 2][:], vu_pad[:, h:h + 1].to_broadcast([P, P]),
                                  kr_feat[:, h // 2, :], start=True, stop=True).then_inc(s_bias, 1)
                    pe.wait_ge(s_biasc, (l + 1) * H + 1)
                    pe.wait_ge(s_split, (l + 1) * 2)
                    weight_turns.wait()
                    with pe.Fori(0, B) as b:
                        it = l * B + b

                        def project_q(p):
                            if p >= 1:
                                pe.wait_ge(s_vc, it * HP + p)
                            w = slice(p * P, (p + 1) * P)
                            three_pass(pe, psA[:], qk_hi[:, w], qk_lo[:, w], x_hi[:], x_lo[:])\
                                .then_inc(s_q, 1)

                        def project_k(p):
                            if p >= 3:
                                pe.wait_ge(s_rc, it * HP + p - 2)
                            w = slice(H * DH + p * P, H * DH + (p + 1) * P)
                            three_pass(pe, psB[:], qk_hi[:, w], qk_lo[:, w], x_hi[:], x_lo[:])\
                                .then_inc(s_k, 1)

                        def project_v(p):
                            pe.wait_ge(s_qlo, it * 2 * HP + 2 * p + 2)
                            for t in range(T):
                                mm = pe.matmul(psA[:, t * P:(t + 1) * P], x_feat[:, t * P:(t + 1) * P],
                                               v_w[:, p * P:(p + 1) * P], start=True, stop=True)
                            mm.then_inc(s_v, 1)

                        def scores(j):
                            p, a, t = j // 8, j % 8 // T, j % T
                            if j % 8 == 0:
                                pe.wait_ge(s_qlo, it * 2 * HP + 2 * p + 2)
                                pe.wait_ge(s_klo, it * HP + p + 1)
                            if j >= 3:
                                pe.wait_ge(s_exp, it * NT + j - 2)
                            w = slice(t * P, (t + 1) * P)
                            three_pass(pe, psS[j % 3][:], q_hi[:, p % 2, a, w], q_lo[:, p % 2, a, w],
                                       k_hi[:, p % 2, :], k_lo[:, p % 2, :]).then_inc(s_S, 1)

                        def transposes(j):
                            pe.wait_ge(s_exp, it * NT + j + 1)
                            if j >= 2:
                                pe.wait_ge((s_ca, s_cv)[j % 2], it * (NT // 2) + j // 2)
                            for n in range(T):
                                mm = pe.transpose(psT[j % 2][:, n * P:(n + 1) * P],
                                                  prob[:, j % 2, n * P:(n + 1) * P], ident[:])
                            mm.then_inc(s_T, 1)

                        def prob_v(p):
                            pe.wait_ge(s_ca, it * (NT // 2) + 4 * p + 4)
                            pe.wait_ge(s_cv, it * (NT // 2) + 4 * p + 4)
                            pe.wait_ge(s_vc, it * HP + p + 1)
                            if p >= 1:
                                pe.wait_ge(s_attn, it * HP + p)
                            for n in range(T):
                                for a in range(2):
                                    r = slice(DH * a, DH * a + DH)
                                    mm = pe.matmul(psV[r, :], v_tok[:, p % 2, n, r],
                                                   prob_t[:, p % 2, a, n, :],
                                                   start=(n == 0), stop=(n == T - 1))
                            mm.then_inc(s_pv, 1)

                        def spread_rec(p):
                            pe.wait_ge(s_rec, it * HP + p + 1)
                            pe.wait_ge(s_ksum, it * HP + min(p + 3, HP))
                            for t in range(T):
                                for a in range(2):
                                    n = a * T + t
                                    mm = pe.matmul(psB[DH * a:DH * a + DH, t * P:(t + 1) * P],
                                                   rec[:, n:n + 1].to_broadcast([P, DH]), ident[:],
                                                   start=True, stop=True)
                            mm.then_inc(s_r, 1)

                        pe.wait_ge(s_x, (it + 1) * 2)
                        project_q(0)
                        project_k(0)
                        project_v(0)
                        scores(0)
                        scores(1)
                        for j in range(NT):
                            p = j // 8
                            if j + 2 < NT:
                                scores(j + 2)
                            transposes(j)
                            if p + 1 < HP:
                                if j % 8 == 0:
                                    project_q(p + 1)
                                if j % 8 == 2:
                                    project_k(p + 1)
                                if j % 8 == 3:
                                    project_v(p + 1)
                            if p >= 1:
                                if j % 8 == 1:
                                    prob_v(p - 1)
                                if j % 8 == 4:
                                    spread_rec(p - 1)
                        prob_v(HP - 1)
                        spread_rec(HP - 1)
                        pe.wait_ge(s_attn, it * HP + HP)
                        for t in range(T):
                            for p in range(HP):
                                mm = pe.matmul(psS0[:, t * P:(t + 1) * P], attn[:, p, t * P:(t + 1) * P],
                                               o_w[:, p, :], start=(p == 0), stop=(p == HP - 1))
                        mm.then_inc(s_o, 1)
                        pe.wait_ge(s_z, it + 1)
                        for t in range(T):
                            mm = pe.transpose(psS1[:, t * P:(t + 1) * P], y[:, t, :], ident[:])
                        mm.then_inc(s_zt, 1)
                        pe.wait_ge(s_zlo, it + 1)
                        for f in range(FB):
                            w = slice(f * P, (f + 1) * P)
                            three_pass(pe, (psA, psB, psT0, psT1)[f][:], f1_hi[:, w], f1_lo[:, w],
                                       x_hi[:], x_lo[:]).then_inc(s_f1, 1)
                        pe.wait_ge(s_f1c, (it + 1) * FB)
                        for t in range(T):
                            for f in range(FB):
                                mm = pe.matmul(psV[:, t * P:(t + 1) * P], ff[:, f, t * P:(t + 1) * P],
                                               f2_w[:, f, :], start=(f == 0), stop=(f == FB - 1))
                        mm.then_inc(s_f2, 1)
                        pe.wait_ge(s_hn, it + 1)
                        for t in range(T):
                            mm = pe.transpose(psS2[:, t * P:(t + 1) * P], y[:, t, :], ident[:])
                        mm.then_inc(s_ht, 1)


def copy_odd(dve, it, j, prob_t, psT, s_T, s_cv):
    p, a, t = j // 8, j % 8 // T, j % T
    dve.wait_ge(s_T, it * NT + j + 1)
    dve.tensor_copy(prob_t[:, p % 2, a, :, t * P:(t + 1) * P],
                    psT[1].rearrange("p (c q) -> p c q", c=T)).then_inc(s_cv, 1)


def experts(nc, ctx, sem, sb_in, bank, ident, h_tok, silu_c, small,
            x, wmod, w1, b1, w2, b2, gate_w, shared_w, shared_b, gamma, beta, out):
    N = B * T
    with ExitStack() as own:
        def sb(name, shape, dt=F32):
            return sb_in(own, name, shape, dt)

        x2 = sb("x2", [P, N, D])
        wm = sb("wm", [P, 4 * D])
        mod = sb("mod", [P, B, 4, D])
        w1_raw = sb("w1_raw", [P, E, DF])
        w2_all = sb("w2_all", [P, E, FB, D])
        b1_all = sb("b1_all", [P, E, FB])
        b2_all = sb("b2_all", [E, D])
        w1_hi = [sb(f"w1_hi{i}", [P, DF], F32R) for i in range(2)]
        w1_lo = [sb(f"w1_lo{i}", [P, DF], F32R) for i in range(2)]
        wg = sb("wg", [P, E])
        ws = sb("ws", [P, D])
        rows3 = sb("rows3", [P, 3, D])
        hm = sb("hm", [P, T, D])
        m_feat = sb("m_feat", [P, S])
        m_hi = sb("m_hi", [P, B * S], F32R)
        m_lo = sb("m_lo", [P, B * S], F32R)
        logit = sb("logit", [P, N, E])
        gsh = sb("gsh", [P, N, D])
        acc = sb("acc", [P, N, D])
        inner = sb("inner", [P, 2, FB, S])
        idx = sb("idx", [P, E])
        pr = sb("pr", [P, N, E])
        top = sb("top", [P, 3, N])
        eq = sb("eq", [P, N, E])
        first = sb("first", [P, N])
        one = sb("one", [P, 2, N, E])
        comb = sb("comb", [P, N, E])
        comb_t = sb("comb_t", [E, N, P])

        s_in, s_iota, s_mod, s_modc = sem("m_in"), sem("m_iota"), sem("m_mod"), sem("m_modc")
        s_ch, s_h, s_tr, s_fe, s_hi, s_lo = (sem("m_ch"), sem("m_h"), sem("m_tr"), sem("m_fe"),
                                             sem("m_hi"), sem("m_lo"))
        s_gate, s_gatec, s_lg, s_e, s_cb, s_ct, s_ctc = (sem("m_gate"), sem("m_gatec"), sem("m_lg"),
                                                         sem("m_e"), sem("m_cb"), sem("m_ct"), sem("m_ctc"))
        s_gelu, s_b2, s_acc = sem("m_gelu"), sem("m_b2"), sem("m_acc")
        s_whi, s_wlo, s_u, s_g, s_y, s_a = (sem("m_whi"), sem("m_wlo"), sem("m_u"), sem("m_g"),
                                            sem("m_y"), sem("m_a"))
        s_out, s_fin = sem("m_out"), sem("m_fin")
        N_IN = 14

        with nc.Block() as block:
            @block.sync
            def _(sp):
                sp.dma_start(wm[:], wmod[:, 2 * D:]).then_inc(s_in, 16)
                sp.dma_start(x2[:], x.rearrange("b (t p) d -> p (b t) d", p=P)).then_inc(s_in, 16)
                sp.dma_start(wg[:], gate_w).then_inc(s_in, 16)
                sp.dma_start(ws[:], shared_w).then_inc(s_in, 16)
                for i, vec in enumerate((shared_b, gamma, beta)):
                    sp.dma_start(rows3[:, i, :], vec.unsqueeze(0).to_broadcast([P, D])).then_inc(s_in, 16)
                sp.dma_start(w1_raw[:], w1.rearrange("e d h -> d e h")).then_inc(s_in, 16)
                for f in range(FB):
                    sp.dma_start(w2_all[:, :, f, :], w2[:, f * P:(f + 1) * P, :].rearrange("e k n -> k e n"))\
                      .then_inc(s_in, 16)
                sp.dma_start(b1_all[:].rearrange("k e f -> k (e f)"),
                             b1.rearrange("e (f k) -> k (e f)", k=P)).then_inc(s_in, 16)
                sp.dma_start(b2_all[:], b2).then_inc(s_in, 16)
                sp.wait_ge(s_fin, B)
                sp.dma_start(out.rearrange("b (t p) d -> p (b t) d", p=P), acc[:]).then_inc(s_out, 16)
                sp.wait_ge(s_out, 16)

            @block.gpsimd
            def _(pool):
                pool.iota(idx[:], pattern=[[1, E]], base=0, channel_multiplier=0,
                          allow_small_or_imprecise_dtypes=True).then_inc(s_iota, 1)
                for n in range(2 * B):
                    inverse_root(pool, small, n + 1)

            @block.scalar
            def _(act):
                for b in range(B):
                    act.wait_ge(s_mod, b + 1)
                    act.activation(mod[:, b].rearrange("p v d -> p (v d)"), bank[b % 2][:], ACT.Copy)\
                       .then_inc(s_modc, 1)
                for b in range(B):
                    act.wait_ge(s_tr, b + 1)
                    act.activation(m_feat[:], bank[2 + b % 2][:], ACT.Copy).then_inc(s_fe, 1)
                    act.activation(m_hi[:, b * S:(b + 1) * S], bank[2 + b % 2][:], ACT.Copy).then_inc(s_hi, 1)
                    act.wait_ge(s_gate, b + 1)
                act.wait_ge(s_lg, 1)
                act.activation(pr[:], logit[:], ACT.Exp).then_inc(s_e, 1)
                act.wait_ge(s_gatec, B)
                act.activation(gsh[:], gsh[:], ACT.Gelu).then_inc(s_gelu, 1)
                up_turns = Turns(act, s_u)
                act.sem_inc(s_g, 1)
                with act.Fori(0, E // 2) as pair:
                    e0 = pair * 2
                    for k in range(2):
                        e = e0 + k
                        if k == 0:
                            act.wait_ge(s_y, e0 * B + 1)
                            for i in range(2):
                                act.activation(w1_hi[i][:], w1_raw[:, e0 + i, :], ACT.Copy).then_inc(s_whi, 1)
                        for g in range(B):
                            for f in range(FB):
                                n = g * FB + f
                                up_turns.wait()
                                act.activation(inner[:, g % 2, f, :], bank[n % 4][:], ACT.Gelu,
                                               bias=b1_all[:, e, f:f + 1]).then_inc(s_g, 1)

            @block.vector
            def _(dve):
                ch, stats = Chain(dve, s_ch), Counted(dve, small[4], T)
                dve.wait_ge(s_in, 16 * N_IN)
                for b in range(B):
                    r = slice(b * T, (b + 1) * T)
                    dve.wait_ge(s_modc, b + 1)
                    for i in (0, 3):
                        ch.link(dve.tensor_scalar(hm[:, i % 2, :], mod[:, b, i, :], 0.0, 2.0, ALU.is_ge,
                                                  ALU.mult))
                        ch.link(dve.scalar_tensor_tensor(out=mod[:, b, i, :], in0=mod[:, b, i, :], scalar=-1.0,
                                                         in1=mod[:, b, i, :], op0=ALU.mult, op1=ALU.max))
                        ch.link(dve.tensor_scalar(mod[:, b, i, :], mod[:, b, i, :], 0.25, None, ALU.max))
                        ch.link(dve.scalar_tensor_tensor(out=mod[:, b, i, :], in0=hm[:, i % 2, :], scalar=-1.0,
                                                         in1=mod[:, b, i, :], op0=ALU.add, op1=ALU.mult))
                    ch.link(dve.tensor_scalar(mod[:, b, 2, :], mod[:, b, 2, :], 1.0, None, ALU.add))
                    ch.link(dve.tensor_tensor(h_tok[:, r, :], h_tok[:, r, :], over_tiles(mod[:, b, 0, :], T),
                                              ALU.mult))
                    ch.link(dve.tensor_tensor(x2[:, r, :], x2[:, r, :], h_tok[:, r, :], ALU.add))
                    if b >= 1:
                        dve.wait_ge(s_tr, b)
                    layer_norm_rows(dve, ch, stats, x2[:, r, :], small, b + 1, hm)
                    ch.link(dve.tensor_tensor(hm[:], hm[:], over_tiles(mod[:, b, 2, :], T), ALU.mult))
                    dve.tensor_tensor(hm[:], hm[:], over_tiles(mod[:, b, 1, :], T), ALU.add).then_inc(s_h, 1)
                    dve.wait_ge(s_hi, b + 1)
                    dve.tensor_tensor(m_lo[:, b * S:(b + 1) * S], bank[2 + b % 2][:],
                                      m_hi[:, b * S:(b + 1) * S].bitcast(F32), ALU.subtract).then_inc(s_lo, 1)
                    dve.wait_ge(s_gate, b + 1)
                    ch.step(dve.tensor_copy(logit[:, r, :],
                                            bank[4][:, 0:T * E].rearrange("p (t e) -> p t e", t=T)))
                    dve.tensor_tensor(gsh[:, r, :], bank[5][:].rearrange("p (t d) -> p t d", t=T),
                                      over_tiles(rows3[:, 0, :], T), ALU.add).then_inc(s_gatec, 1)

                def wide(a):
                    return a.unsqueeze(2).to_broadcast([P, N, E])

                idxs = idx[:].unsqueeze(1).to_broadcast([P, N, E])
                ch.wait()
                ch.link(dve.tensor_reduce(top[:, 0, :], logit[:], AX.X, ALU.max))
                dve.tensor_tensor(logit[:], logit[:], wide(top[:, 0, :]), ALU.subtract).then_inc(s_lg, 1)
                dve.wait_ge(s_e, 1)
                ch.link(dve.tensor_reduce(top[:, 2, :], pr[:], AX.X, ALU.add))
                ch.link(dve.reciprocal(top[:, 2, :], top[:, 2, :]))
                ch.link(dve.tensor_tensor(pr[:], pr[:], wide(top[:, 2, :]), ALU.mult))
                dve.wait_ge(s_iota, 1)
                for k in range(2):
                    ch.link(dve.tensor_reduce(top[:, k, :], pr[:], AX.X, ALU.max))
                    ch.link(dve.tensor_tensor(eq[:], pr[:], wide(top[:, k, :]), ALU.is_equal))
                    ch.link(dve.tensor_scalar(eq[:], eq[:], -float(E), float(E), ALU.mult, ALU.add))
                    ch.link(dve.tensor_tensor(eq[:], eq[:], idxs, ALU.add))
                    ch.link(dve.tensor_reduce(first[:], eq[:], AX.X, ALU.min))
                    ch.link(dve.tensor_tensor(one[:, k], idxs, wide(first[:]), ALU.is_equal))
                    if k == 0:
                        ch.link(dve.scalar_tensor_tensor(out=pr[:], in0=one[:, 0], scalar=-2.0, in1=pr[:],
                                                         op0=ALU.mult, op1=ALU.add))
                ch.link(dve.tensor_tensor(top[:, 2, :], top[:, 0, :], top[:, 1, :], ALU.add))
                ch.link(dve.reciprocal(top[:, 2, :], top[:, 2, :]))
                for k in range(2):
                    ch.link(dve.tensor_tensor(top[:, k, :], top[:, k, :], top[:, 2, :], ALU.mult))
                    ch.link(dve.tensor_tensor(one[:, k], one[:, k], wide(top[:, k, :]), ALU.mult))
                dve.tensor_tensor(comb[:], one[:, 0], one[:, 1], ALU.add).then_inc(s_cb, 1)
                for g in range(B):
                    dve.wait_ge(s_ct, g + 1)
                    dve.tensor_copy(comb_t[:, g * T:(g + 1) * T, :],
                                    bank[6][0:E, :].rearrange("e (t p) -> e t p", t=T)).then_inc(s_ctc, 1)
                dve.wait_ge(s_gelu, 1)
                for g in range(B):
                    dve.wait_ge(s_b2, g + 1)
                    dve.scalar_tensor_tensor(out=acc[:, g * T:(g + 1) * T, :], in0=gsh[:, g * T:(g + 1) * T, :],
                                             scalar=0.5, in1=bank[7][:].rearrange("p (t d) -> p t d", t=T),
                                             op0=ALU.mult, op1=ALU.add).then_inc(s_acc, 1)
                dve.wait_ge(s_acc, B)
                dve.sem_inc(s_a, 1)
                with dve.Fori(0, E // 2) as pair:
                    e0 = pair * 2
                    for k in range(2):
                        e = e0 + k
                        if k == 0:
                            dve.wait_ge(s_whi, e0 + 2)
                            for i in range(2):
                                dve.tensor_tensor(w1_lo[i][:], w1_raw[:, e0 + i, :],
                                                  w1_hi[i][:].bitcast(F32), ALU.subtract).then_inc(s_wlo, 1)
                        for g in range(B):
                            dve.wait_ge(s_y, e * B + g + 2)
                            for t in range(T):
                                n = g * T + t
                                if n == 0:
                                    dve.wait_ge(s_a, e * N + 1)
                                dve.scalar_tensor_tensor(
                                    out=acc[:, n, :], in0=bank[4 + g % 2][:, t * P:(t + 1) * P],
                                    scalar=comb[:, n, bass.ds(e, 1)], in1=acc[:, n, :],
                                    op0=ALU.mult, op1=ALU.add).then_inc(s_a, 1)
                dve.wait_ge(s_a, E * N + 1)
                for b in range(B):
                    r = slice(b * T, (b + 1) * T)
                    rows = acc[:, r, :]
                    layer_norm_rows(dve, ch, stats, rows, small, B + b + 1, rows)
                    ch.link(dve.tensor_tensor(rows, rows, over_tiles(rows3[:, 1, :], T), ALU.mult))
                    ch.link(dve.tensor_tensor(rows, rows, over_tiles(rows3[:, 2, :], T), ALU.add))
                    ch.link(dve.tensor_tensor(rows, rows, over_tiles(mod[:, b, 3, :], T), ALU.mult))
                    dve.tensor_tensor(rows, rows, x2[:, r, :], ALU.add).then_inc(s_fin, 1)

            @block.tensor
            def _(pe):
                pe.wait_ge(s_in, 16 * N_IN)
                for b in range(B):
                    if b >= 2:
                        pe.wait_ge(s_modc, b - 1)
                    pe.matmul(bank[b % 2][:], silu_c[:, b:b + 1].to_broadcast([P, P]), wm[:],
                              start=True, stop=True).then_inc(s_mod, 1)
                for b in range(B):
                    pe.wait_ge(s_h, b + 1)
                    for t in range(T):
                        mm = pe.transpose(bank[2 + b % 2][:, t * P:(t + 1) * P], hm[:, t, :], ident[:])
                    mm.then_inc(s_tr, 1)
                    pe.wait_ge(s_fe, b + 1)
                    if b >= 1:
                        pe.wait_ge(s_gatec, b)
                    for t in range(T):
                        pe.matmul(bank[4][:, t * E:(t + 1) * E], m_feat[:, t * P:(t + 1) * P], wg[:],
                                  start=True, stop=True)
                        mm = pe.matmul(bank[5][:, t * P:(t + 1) * P], m_feat[:, t * P:(t + 1) * P], ws[:],
                                       start=True, stop=True)
                    mm.then_inc(s_gate, 1)
                pe.wait_ge(s_cb, 1)
                for g in range(B):
                    if g >= 1:
                        pe.wait_ge(s_ctc, g)
                    for t in range(T):
                        mm = pe.transpose(bank[6][0:E, t * P:(t + 1) * P], comb[:, g * T + t, :], ident[:])
                    mm.then_inc(s_ct, 1)
                for g in range(B):
                    pe.wait_ge(s_ctc, g + 1)
                    if g >= 1:
                        pe.wait_ge(s_acc, g)
                    for t in range(T):
                        mm = pe.matmul(bank[7][:, t * P:(t + 1) * P], comb_t[:, g * T + t, :], b2_all[:],
                                       start=True, stop=True)
                    mm.then_inc(s_b2, 1)
                pe.wait_ge(s_lo, B)
                pe.sem_inc(s_y, 1)
                with pe.Fori(0, E // 2) as pair:
                    e0 = pair * 2
                    pe.wait_ge(s_wlo, e0 + 2)
                    for k in range(2):
                        e = e0 + k

                        def up(g):
                            for f in range(FB):
                                n = g * FB + f
                                if n >= 4:
                                    pe.wait_ge(s_g, e * B * FB + n - 2)
                                else:
                                    pe.wait_ge(s_g, e * B * FB + 1)
                                w = slice(f * P, (f + 1) * P)
                                m = slice(g * S, (g + 1) * S)
                                pe.matmul(bank[n % 4][:], w1_hi[k][:, w], m_hi[:, m], start=True, stop=False)
                                pe.matmul(bank[n % 4][:], w1_hi[k][:, w], m_lo[:, m], start=False, stop=False)
                                pe.matmul(bank[n % 4][:], w1_lo[k][:, w], m_hi[:, m], start=False, stop=True)\
                                    .then_inc(s_u, 1)

                        def down(g):
                            pe.wait_ge(s_g, e * B * FB + (g + 1) * FB + 1)
                            if g >= 2:
                                pe.wait_ge(s_a, e * N + (g - 1) * T + 1)
                            else:
                                pe.wait_ge(s_a, e * N + 1)
                            for t in range(T):
                                for f in range(FB):
                                    mm = pe.matmul(bank[4 + g % 2][:, t * P:(t + 1) * P],
                                                   inner[:, g % 2, f, t * P:(t + 1) * P],
                                                   w2_all[:, e, f, :], start=(f == 0), stop=(f == FB - 1))
                            mm.then_inc(s_y, 1)

                        up(0)
                        for g in range(B):
                            if g + 1 < B:
                                up(g + 1)
                            down(g)


_INS = ['L0_attn_x', 'L0_attn_W_qkv', 'L0_attn_W_r', 'L0_attn_W_o', 'L0_attn_u', 'L0_attn_v',
        'L0_attn_ln1_g', 'L0_attn_ln1_b', 'L0_attn_W_ff1', 'L0_attn_b_ff1', 'L0_attn_W_ff2',
        'L0_attn_b_ff2', 'L0_attn_ln2_g', 'L0_attn_ln2_b', 'L0_ffn_W1', 'L0_ffn_b1', 'L0_ffn_W2',
        'L0_ffn_b2', 'L0_ffn_gate_W', 'L0_ffn_shared_W', 'L0_ffn_shared_b', 'L0_ffn_gamma',
        'L0_ffn_beta', 'L0_c', 'L0_wmod']


def kernel(**inputs):
    import numpy as _np
    import concourse.bacc as _bacc
    from concourse import mybir as _mybir
    from concourse.bass_utils import run_bass_kernel_spmd as _run

    nc = _bacc.Bacc("TRN2", target_bir_lowering=False, num_devices=1)
    arrays, args = {}, []
    for name in _INS:
        a = _np.ascontiguousarray(inputs[name])
        arrays[f"in_{name}"] = a
        args.append(nc.dram_tensor(f"in_{name}", a.shape, _mybir.dt.from_np(a.dtype),
                                   kind="ExternalInput").ap())
    at = _np.arange(S - 1, -1, -1, dtype=_np.float32)
    freq = (_np.float32(1.0) / _np.float32(10000.0)
            ** (_np.arange(0, D, 2, dtype=_np.float32) / _np.float32(D))).astype(_np.float32)
    ang = freq[:, None] * at[None, :]
    arrays["pos_t"] = _np.concatenate([_np.sin(ang), _np.cos(ang)], axis=0).astype(_np.float32)
    args.append(nc.dram_tensor("pos_t", (D, S), _mybir.dt.float32, kind="ExternalInput").ap())
    args.append(nc.dram_tensor("out_0", (B, S, D), _mybir.dt.float32, kind="ExternalOutput").ap())
    build(nc, *args)
    r = _run(nc, [arrays], core_ids=[0])
    return r.results[0]["out_0"]
```

```python
import concourse.bass as bass
from concourse import mybir
from contextlib import ExitStack

F32 = mybir.dt.float32
F32R = mybir.dt.float32r
ALU = mybir.AluOpType
ACT = mybir.ActivationFunctionType
AX = mybir.AxisListType

P = 128
B = 4
S = 512
D = 128
T = S // P
L = 4
H = 16
DH = 64
HP = H // 2
DF = 512
FB = DF // P
E = 8
NT = HP * 2 * T
EPS = 1e-5
SCALE = DH ** -0.5
N_MOD = 6
SA, CA, GA, SB_, CB, GB = range(N_MOD)


class Turns:

    def __init__(self, eng, sem, start=1, step=1):
        self.eng, self.sem, self.by = eng, sem, step
        self.count = eng.alloc_register(f"turn_{sem.name}")
        eng.reg_mov(self.count, start)

    def wait(self):
        self.eng.wait_ge(self.sem, self.count)
        self.eng.reg_add(self.count, self.count, self.by)


class Counted:

    def __init__(self, eng, sem, step, n=0):
        self.eng, self.sem, self.by, self.n = eng, sem, step, n

    def wait(self):
        self.n += self.by
        self.eng.wait_ge(self.sem, self.n)


class Chain:

    def __init__(self, eng, sem, base=0):
        self.eng, self.sem, self.base, self.n = eng, sem, base, 0

    def step(self, ins):
        self.n += 1
        ins.then_inc(self.sem, 1)

    def wait(self):
        self.eng.wait_ge(self.sem, self.base + self.n)

    def link(self, ins):
        self.step(ins)
        self.wait()


def layer_norm_rows(dve, chain, stats, src, small, count, dst):
    n, (stat, mv, rstd, _, s_stat, s_var, s_rstd) = T, small
    for t in range(n):
        dve.bn_stats(stat[:, t, :], src[:, t, :]).then_inc(s_stat, 1)
    stats.wait()
    for t in range(n):
        chain.step(dve.bn_aggr(mv[:, t, :], stat[:, t, :]))
    chain.wait()
    dve.tensor_scalar(rstd[:], mv[:, :, 1], EPS, None, ALU.add).then_inc(s_var, 1)
    dve.wait_ge(s_rstd, count)
    for t in range(n):
        chain.step(dve.tensor_scalar(dst[:, t, :], src[:, t, :], mv[:, t, 0:1], rstd[:, t:t + 1],
                                     ALU.subtract, ALU.mult))
    chain.wait()


LN_STEPS = 2 * T


def inverse_root(pool, small, count):
    _, _, rstd, exponent, _, s_var, s_rstd = small
    pool.wait_ge(s_var, count)
    pool.tensor_tensor(rstd[:], rstd[:], exponent[:], ALU.pow).then_inc(s_rstd, 1)


def over_tiles(row, n):
    return row.unsqueeze(1).to_broadcast([P, n, D])


def build(nc, x, w_qkv, w_r, w_o, u, v, ln1_g, ln1_b, w_ff1, b_ff1, w_ff2, b_ff2, ln2_g, ln2_b,
          w1, b1, w2, b2, gate_w, shared_w, shared_b, gamma, beta, c, wmod, pos_t, out):
    ctx = ExitStack()
    with ctx:
        ctx.enter_context(nc.allow_non_contiguous_dma(reason="small transposed loads of vectors"))

        def sem(name):
            return ctx.enter_context(nc.semaphore(name))

        def sb_in(stack, name, shape, dt=F32):
            return stack.enter_context(nc.sbuf_tensor(name, shape, dt))

        def sb(name, shape, dt=F32):
            return sb_in(ctx, name, shape, dt)

        bank = [ctx.enter_context(nc.psum_tensor(f"bank{i}", [P, 512], F32)) for i in range(8)]

        ident = sb("ident", [P, P])
        h_tok = sb("h_tok", [P, (B + 1) * T, D])
        h_feat = sb("h_feat", [P, B + 1, S])
        silu_c = sb("silu_c", [P, B])
        stat = sb("stat", [P, T, 6])
        mv = sb("mv", [P, T, 2])
        rstd = sb("rstd", [P, T])
        exponent = sb("exponent", [P, T])
        small = [(stat, mv, rstd, exponent, sem(f"stat{i}"), sem(f"var{i}"), sem(f"rstd{i}")) for i in range(3)]

        modulate_in(nc, ctx, sem, sb_in, bank, ident, h_tok, h_feat, silu_c, small[0],
                    x, c, wmod)
        transformer(nc, ctx, sem, sb_in, bank, ident, h_tok, h_feat, small[1],
                    w_qkv, w_r, w_o, u, v, ln1_g, ln1_b, w_ff1, b_ff1, w_ff2, b_ff2, ln2_g, ln2_b,
                    pos_t)
        experts(nc, ctx, sem, sb_in, bank, ident, h_tok, silu_c, small[2],
                x, wmod, w1, b1, w2, b2, gate_w, shared_w, shared_b, gamma, beta, out)


def modulate_in(nc, ctx, sem, sb_in, bank, ident, h_tok, h_feat, silu_c, small, x, c, wmod):
    with ExitStack() as own:
        c_feat = sb_in(own, "c_feat", [P, B])
        wm = sb_in(own, "wm_in", [P, 2 * D])
        x_in = sb_in(own, "x_in", [P, B * T, D])
        mod = sb_in(own, "mod_in", [P, B, 2 * D])
        s_id, s_x, s_c, s_wm = sem("in_ident"), sem("in_x"), sem("in_c"), sem("in_wm")
        s_exp, s_silu, s_mod, s_modc = sem("in_exp"), sem("in_silu"), sem("in_mod"), sem("in_modc")
        s_chain, s_h, s_tr, s_tc = sem("in_chain"), sem("in_h"), sem("in_tr"), sem("in_tc")

        with nc.Block() as block:
            @block.sync
            def _(sp):
                sp.dma_start(c_feat[:], c.rearrange("b d -> d b")).then_inc(s_c, 16)
                sp.dma_start(wm[:], wmod[:, 0:2 * D]).then_inc(s_wm, 16)
                sp.dma_start(x_in[:], x.rearrange("b (t p) d -> p (b t) d", p=P)).then_inc(s_x, 16)

            @block.gpsimd
            def _(pool):
                pool.memset(ident[:], 0.0).then_inc(s_id, 1)
                pool.wait_ge(s_id, 1)
                pool.affine_select(out=ident[:], in_=ident[:], compare_op=ALU.not_equal, fill=1.0,
                                   base=0, pattern=[[-1, P]], channel_multiplier=1).then_inc(s_id, 1)
                pool.memset(small[3][:], -0.5).then_inc(s_id, 1)
                pool.wait_ge(s_id, 3)
                for b in range(B):
                    inverse_root(pool, small, b + 1)

            @block.scalar
            def _(act):
                act.wait_ge(s_c, 16)
                act.activation(silu_c[:], c_feat[:], ACT.Exp, scale=-1.0).then_inc(s_exp, 1)
                for b in range(B):
                    act.wait_ge(s_mod, b + 1)
                    act.activation(mod[:, b, :], bank[b][:, 0:2 * D], ACT.Copy).then_inc(s_modc, 1)
                for b in range(B):
                    act.wait_ge(s_tr, b + 1)
                    act.activation(h_feat[:, b, :], bank[4 + b][:], ACT.Copy).then_inc(s_tc, 1)

            @block.vector
            def _(dve):
                ch, stats = Chain(dve, s_chain), Counted(dve, small[4], T)
                dve.wait_ge(s_exp, 1)
                ch.link(dve.tensor_scalar(silu_c[:], silu_c[:], 1.0, None, ALU.add))
                ch.link(dve.reciprocal(silu_c[:], silu_c[:]))
                dve.tensor_tensor(silu_c[:], silu_c[:], c_feat[:], ALU.mult).then_inc(s_silu, 1)
                dve.wait_ge(s_x, 16)
                for b in range(B):
                    rows = h_tok[:, b * T:(b + 1) * T, :]
                    layer_norm_rows(dve, ch, stats, x_in[:, b * T:(b + 1) * T, :], small, b + 1, rows)
                    dve.wait_ge(s_modc, b + 1)
                    ch.link(dve.tensor_scalar(mod[:, b, D:2 * D], mod[:, b, D:2 * D], 1.0, None, ALU.add))
                    ch.link(dve.tensor_tensor(rows, rows, over_tiles(mod[:, b, D:2 * D], T), ALU.mult))
                    dve.tensor_tensor(rows, rows, over_tiles(mod[:, b, 0:D], T), ALU.add)\
                       .then_inc(s_h, 1)

            @block.tensor
            def _(pe):
                pe.wait_ge(s_silu, 1)
                pe.wait_ge(s_wm, 16)
                for b in range(B):
                    pe.matmul(bank[b][:, 0:2 * D], silu_c[:, b:b + 1].to_broadcast([P, P]), wm[:],
                              start=True, stop=True).then_inc(s_mod, 1)
                pe.wait_ge(s_id, 2)
                for b in range(B):
                    pe.wait_ge(s_h, b + 1)
                    for t in range(T):
                        mm = pe.transpose(bank[4 + b][:, t * P:(t + 1) * P], h_tok[:, b * T + t, :],
                                          ident[:])
                    mm.then_inc(s_tr, 1)


def transformer(nc, ctx, sem, sb_in, bank, ident, h_tok, h_feat, small,
                w_qkv, w_r, w_o, u, v, ln1_g, ln1_b, w_ff1, b_ff1, w_ff2, b_ff2, ln2_g, ln2_b, pos_t):
    with ExitStack() as own:
        def sb(name, shape, dt=F32):
            return sb_in(own, name, shape, dt)

        qk_hi = sb("qk_hi", [P, 2 * H * DH], F32R)
        qk_lo = sb("qk_lo", [P, 2 * H * DH], F32R)
        vw_hi = sb("vw_hi", [P, H * DH], F32R)
        vw_lo = sb("vw_lo", [P, H * DH], F32R)
        o_w = sb("o_w", [P, HP, D])
        f1_w = sb("f1_w", [P, DF])
        f2_w = sb("f2_w", [P, FB, D])
        rows = sb("rows", [P, 5, D])
        f1_b = sb("f1_b", [P, FB])
        pos = sb("pos", [P, S])
        u_col = sb("u_col", [P, HP])
        v_col = sb("v_col", [P, HP])
        vu_pad = sb("vu_pad", [P, H])
        kr_feat = sb("kr_feat", [P, HP, S])
        kr_bias = sb("kr_bias", [P, H, S])
        N_PROB = 4
        AHEAD = 3
        x_hi = sb("x_hi", [P, S], F32R)
        x_lo = sb("x_lo", [P, S], F32R)
        q_st = sb("q_st", [P, 2, 2, S], F32R)
        k_sum = sb("k_sum", [P, S])
        k_hi = sb("k_hi", [P, 2, 2, S], F32R)
        k_lo = sb("k_lo", [P, 2, 2, S], F32R)
        v_tok = sb("v_tok", [P, T, HP // 2 * P])
        neg_max = sb("neg_max", [P, N_PROB])
        sums = sb("sums", [P, 2, 2 * T])
        rec = sb("rec", [P, 2 * T])
        rec_wide = sb("rec_wide", [P, T, 2, DH])
        rec_row = sb("rec_row", [P, S])
        prob = sb("prob", [P, N_PROB, S])
        prob_t = sb("prob_t", [P, 2, 2, T, S])
        attn = sb("attn", [P, HP, S])
        y = sb("y", [P, T, D])
        z_feat = sb("z_feat", [P, S])
        landing = prob_t[:, 0].rearrange("p a c q -> p (a c q)")
        qk_raw = landing[:, 0:2 * H * DH]
        v_raw = landing[:, 2 * H * DH:3 * H * DH]
        r_raw = landing[:, 3 * H * DH:4 * H * DH]
        ff = attn[:, HP // 2:, :]

        (psS0, psS1, psS2, psT0, psT1, psV, psA, psB) = bank
        psS, psT = (psS0, psS1, psS2), (psT0, psT1)
        halves = (slice(0, DH), slice(DH, P))
        v_at = {(4, 5): (4,), (4, 6): (5, 6), (4, 7): (7,)}
        v_bank = (psT0, psT1, psA, psS2, psA, psB, psA, psA)
        ff1_at = {(2, 6): (0, 1), (3, 5): (2,), (3, 6): (3,)}

        s_const, s_rin, s_raw, s_w, s_uv, s_zero = (sem("const"), sem("r_in"), sem("raw_in"), sem("w_in"),
                                                    sem("uv"), sem("zero"))
        s_split_hi, s_split = sem("split_hi"), sem("split")
        s_kr, s_krc, s_bias, s_biasc = sem("kr"), sem("krc"), sem("bias"), sem("biasc")
        s_xhi, s_xlo = sem("x_hi"), sem("x_lo")
        s_q, s_qhi, s_qlo = sem("q"), sem("q_hi"), sem("q_lo")
        s_k, s_ksum, s_khi, s_kdup, s_klo = sem("k"), sem("k_sum"), sem("k_hi"), sem("k_dup"), sem("k_lo")
        s_v, s_vc = sem("v"), sem("vc")
        s_S, s_max, s_exp = sem("scores"), sem("max"), sem("exp")
        s_T, s_ca, s_cv = sem("probT"), sem("copied_act"), sem("copied_dve")
        s_pv, s_rec, s_wide, s_r, s_rc, s_attn = (sem("pv"), sem("rec"), sem("rec_wide"), sem("r"),
                                                  sem("rc"), sem("attn"))
        s_o, s_y1, s_norm, s_g, s_z, s_zt, s_zc = (sem("o"), sem("y1"), sem("norm"), sem("ln_g"), sem("z"),
                                                   sem("zt"), sem("zc"))
        s_f1, s_f1c, s_f2, s_y2, s_hn, s_ht, s_done, s_res = (
            sem("f1"), sem("f1c"), sem("f2"), sem("y2"), sem("hn"), sem("ht"), sem("done"), sem("res"))
        s_ch = sem("dve_chain")
        N_W = 9
        s_stat, s_var, s_rstd = small[4:7]

        def tail_weights(it):
            return ((it + B - 1) // B + 1) * 16 * N_W

        def three_pass(pe, ps, w_hi, w_lo, m_hi, m_lo):
            pe.matmul(ps, w_hi, m_hi, start=True, stop=False)
            pe.matmul(ps, w_hi, m_lo, start=False, stop=False)
            return pe.matmul(ps, w_lo, m_hi, start=False, stop=True)

        with nc.Block() as block:
            @block.sync
            def _(sp):
                def load_o(l):
                    sp.dma_start(o_w[:], w_o[l].rearrange("(p k) n -> k p n", k=P)).then_inc(s_w, 16)

                def load_f1(l):
                    sp.dma_start(f1_w[:], w_ff1[l]).then_inc(s_w, 16)
                    sp.dma_start(f1_b[:], b_ff1[l].rearrange("(f k) -> k f", k=P)).then_inc(s_w, 16)

                def load_f2(l):
                    sp.dma_start(f2_w[:], w_ff2[l].rearrange("(f k) n -> k f n", k=P)).then_inc(s_w, 16)

                def load_rows(l):
                    for i, vec in enumerate((ln1_g, ln1_b, ln2_g, ln2_b, b_ff2)):
                        sp.dma_start(rows[:, i, :], vec[l].unsqueeze(0).to_broadcast([P, D]))\
                          .then_inc(s_w, 16)

                sp.dma_start(pos[:], pos_t).then_inc(s_const, 16)
                sp.dma_start(u_col[:], u.rearrange("(p two) d -> (two d) p", two=2)).then_inc(s_const, 16)
                sp.dma_start(v_col[:], v.rearrange("(p two) d -> (two d) p", two=2)).then_inc(s_const, 16)
                load_o(0)
                load_f1(0)
                load_f2(0)
                load_rows(0)
                with sp.Fori(0, L) as l:
                    it = l * B
                    sp.wait_ge(s_pv, it * HP + 1)
                    sp.dma_start(r_raw, w_r[l]).then_inc(s_rin, 16)
                    sp.dma_start(qk_raw, w_qkv[l, :, 0:2 * H * DH]).then_inc(s_raw, 16)
                    sp.dma_start(v_raw, w_qkv[l, :, 2 * H * DH:]).then_inc(s_raw, 16)
                    sp.wait_ge(s_o, it + 1)
                    load_o(l)
                    sp.wait_ge(s_f1c, (it + 1) * FB)
                    load_f1(l)
                    sp.wait_ge(s_f2, it + 1)
                    load_f2(l)
                    sp.wait_ge(s_hn, it + 1)
                    load_rows(l)

            @block.gpsimd
            def _(pool):
                prev = pool.alloc_register("prev_pool")
                pool.reg_mov(prev, B)
                klo_turns = Turns(pool, s_klo, 4, 4)
                rec_turns, r_turns, hn_turns = Turns(pool, s_rec), Turns(pool, s_r), Turns(pool, s_hn)
                for t in (vu_pad[:], v_tok[:], h_tok[:, B * T:, :]):
                    pool.memset(t, 0.0).then_inc(s_zero, 1)
                pool.memset(rec_wide[:], 0.0).then_inc(s_wide, 1)
                pool.sem_inc(s_res, 1)

                def k_low(it, p):
                    pool.wait_ge(s_khi, (it * HP + p + 1) * 2)
                    for i in range(4):
                        a, r, to = i // 2, halves[i // 2], halves[(i + 1) // 2 % 2]
                        if i >= 1:
                            pool.wait_ge(s_klo, (it * HP + p) * 4 + i)
                        pool.tensor_tensor(k_lo[to, p % 2, a, :], k_sum[r, :],
                                           k_hi[r, p % 2, a, :].bitcast(F32), ALU.subtract)\
                            .then_inc(s_klo, 1)
                    klo_turns.wait()

                def widen():
                    rec_turns.wait()
                    r_turns.wait()
                    pool.tensor_copy(rec_wide[:], rec[:].rearrange("p (a t) -> p t a", t=T).unsqueeze(3)
                                     .to_broadcast([P, T, 2, DH])).then_inc(s_wide, 1)

                def normalise_rows(count, g, b_row, done):
                    pool.wait_ge(s_var, count)
                    pool.tensor_tensor(small[2][:], small[2][:], small[3][:], ALU.pow).then_inc(s_rstd, 1)
                    pool.wait_ge(s_norm, count * T)
                    pool.tensor_tensor(y[:], y[:], over_tiles(rows[:, g, :], T), ALU.mult).then_inc(s_g, 1)
                    pool.wait_ge(s_g, count)
                    pool.tensor_tensor(y[:], y[:], over_tiles(rows[:, b_row, :], T), ALU.add).then_inc(done, 1)

                def residual(slot, hn_turns=hn_turns):
                    hn_turns.wait()
                    pool.tensor_copy(h_tok[:, bass.ts(slot, T), :], y[:]).then_inc(s_res, 1)

                with pool.Fori(0, L) as l:
                    pool.wait_ge(s_split_hi, (l + 1) * 2)
                    pool.tensor_tensor(qk_lo[:], qk_raw, qk_hi[:].bitcast(F32), ALU.subtract)\
                        .then_inc(s_split, 1)
                    pool.tensor_tensor(vw_lo[:], v_raw, vw_hi[:].bitcast(F32), ALU.subtract)\
                        .then_inc(s_split, 1)
                    with pool.Fori(0, B) as b:
                        it = l * B + b
                        pool.wait_ge(s_w, tail_weights(it))
                        k_low(it, 0)
                        for w in range(HP):
                            if w >= 1:
                                widen()
                            if w + 1 < HP:
                                k_low(it, w + 1)
                            if w == 1:
                                normalise_rows(it * 2 + 1, 0, 1, s_z)
                            if w == 6:
                                normalise_rows(it * 2 + 2, 2, 3, s_hn)
                            if w == 7:
                                residual(pool.snap(prev, min_val=0, max_val=B))
                        widen()
                        pool.reg_mov(prev, b)
                it = L * B
                normalise_rows(it * 2 + 1, 0, 1, s_z)
                normalise_rows(it * 2 + 2, 2, 3, s_hn)
                residual(B - 1, Counted(pool, s_hn, 1, it))

            @block.scalar
            def _(act):
                prev = act.alloc_register("prev_act")
                act.reg_mov(prev, B)
                done_turns, ht_turns = Turns(act, s_done), Turns(act, s_ht)
                act.sem_inc(s_done, 1)
                act.sem_inc(s_rc, 1)
                act.activation(x_hi[:], h_feat[:, 0, :], ACT.Copy).then_inc(s_xhi, 1)

                def q_high(it, p):
                    act.wait_ge(s_q, it * HP + p + 1)
                    for a, r in enumerate(halves):
                        act.activation(q_st[r, p % 2, a, :], psA[r, :], ACT.Identity,
                                       bias=u_col[r, p:p + 1]).then_inc(s_qhi, 1)

                def k_double(it, p):
                    for a, r in enumerate(halves):
                        act.wait_ge(s_khi, (it * HP + p) * 2 + a + 1)
                        act.activation(k_hi[halves[1 - a], p % 2, a, :], k_hi[r, p % 2, a, :].bitcast(F32),
                                       ACT.Copy).then_inc(s_kdup, 1)

                def v_out(it, n, ps):
                    act.wait_ge(s_v, it * 2 * T + n + 1)
                    act.activation(v_tok[:, n % T, :], ps[:], ACT.Copy).then_inc(s_vc, 1)

                def r_out(it, w):
                    act.wait_ge(s_r, it * HP + w + 1)
                    act.wait_ge(s_attn, it * HP + w + 1)
                    act.activation(rec_row[:], psB[:], ACT.Copy).then_inc(s_rc, 1)

                def exponential(it, j):
                    act.wait_ge(s_max, it * NT + j + 1)
                    w = j // 8
                    act.activation(prob[:, j % N_PROB, :], prob[:, j % N_PROB, :], ACT.Exp, scale=-1.0,
                                   bias=neg_max[:, j % N_PROB:j % N_PROB + 1],
                                   accum_out=sums[:, w % 2, j % 8:j % 8 + 1]).then_inc(s_exp, 1)

                def copy_even(it, j):
                    w, a, t = j // 8, j % 8 // T, j % T
                    act.wait_ge(s_T, it * NT + j + 1)
                    act.activation(prob_t[:, w % 2, a, :, t * P:(t + 1) * P],
                                   psT[0].rearrange("p (c q) -> p c q", c=T), ACT.Copy).then_inc(s_ca, 1)

                def z_out(it):
                    act.wait_ge(s_zt, it + 1)
                    act.activation(z_feat[:], psA[:], ACT.Copy).then_inc(s_zc, 1)

                def relu(it, f):
                    act.wait_ge(s_f1, it * FB + f + 1)
                    act.activation(ff[:, f, :], (psA, psB)[f % 2][:], ACT.Relu, bias=f1_b[:, f:f + 1])\
                        .then_inc(s_f1c, 1)

                with act.Fori(0, L) as l:
                    for p in range(HP):
                        act.wait_ge(s_kr, l * HP + p + 1)
                        act.activation(kr_feat[:, p, :], psS[p % 2][:], ACT.Copy).then_inc(s_krc, 1)
                    act.wait_ge(s_raw, (l + 1) * 32)
                    act.activation(qk_hi[:], qk_raw, ACT.Copy).then_inc(s_split_hi, 1)
                    act.activation(vw_hi[:], v_raw, ACT.Copy).then_inc(s_split_hi, 1)
                    with act.Fori(0, B) as b:
                        it = l * B + b
                        act.wait_ge(s_w, tail_weights(it))
                        q_high(it, 0)
                        k_double(it, 0)
                        act.wait_ge(s_pv, it * HP + 2)
                        for n in range(T):
                            v_out(it, n, v_bank[n])
                        r_out(it, 0)
                        for j in range(AHEAD):
                            exponential(it, j)
                        for j in range(NT):
                            w, s = j // 8, j % 8
                            if j % 2 == 0:
                                copy_even(it, j)
                            if j + AHEAD < NT:
                                exponential(it, j + AHEAD)
                            if s == 1 and w + 1 < HP:
                                q_high(it, w + 1)
                            if s == 2 and w + 1 < HP:
                                k_double(it, w + 1)
                            if s == 4 and w >= 1:
                                r_out(it, w)
                            if (w, s) == (2, 4):
                                z_out(it)
                            for f in ff1_at.get((w, s), ()):
                                relu(it, f)
                            for n in v_at.get((w, s), ()):
                                act.wait_ge(s_pv, it * HP + 6)
                                v_out(it, n, v_bank[n])
                            if (w, s) == (7, 1):
                                done_turns.wait()
                                act.activation(x_hi[:], h_feat[:, (b + 1) % B, :], ACT.Copy).then_inc(s_xhi, 1)
                            if (w, s) == (7, 5):
                                ht_turns.wait()
                                act.activation(h_feat[:, act.snap(prev, min_val=0, max_val=B), :], psA[:],
                                               ACT.Copy).then_inc(s_done, 1)
                        act.reg_mov(prev, b)
                it = L * B
                r_out(it, 0)
                z_out(it)
                for f in range(FB):
                    relu(it, f)

            @block.vector
            def _(dve):
                prev = dve.alloc_register("prev_dve")
                dve.reg_mov(prev, B)
                score_turns, stats = Turns(dve, s_S), Turns(dve, s_stat, T, T)
                rstd_turns = Turns(dve, s_rstd)
                dve.memset(prob_t[:, 1], 0.0).then_inc(s_ca, 1)
                dve.memset(attn[:], 0.0).then_inc(s_cv, 1)
                dve.wait_ge(s_xhi, 1)
                dve.tensor_tensor(x_lo[:], h_feat[:, 0, :], x_hi[:].bitcast(F32), ALU.subtract)\
                    .then_inc(s_xlo, 1)
                dve.wait_ge(s_const, 48)
                dve.wait_ge(s_zero, 3)
                for a, r in enumerate(halves):
                    dve.tensor_tensor(vu_pad[r, a::2], v_col[r, :], u_col[r, :], ALU.subtract)\
                       .then_inc(s_uv, 1)
                dve.sem_inc(s_biasc, 1)
                dve.sem_inc(s_attn, 1)

                def q_low(it, p):
                    for a, r in enumerate(halves):
                        dve.wait_ge(s_qhi, (it * HP + p) * 2 + a + 1)
                        dve.scalar_tensor_tensor(out=q_st[halves[1 - a], p % 2, a, :], in0=psA[r, :],
                                                 scalar=u_col[r, p:p + 1],
                                                 in1=q_st[r, p % 2, a, :].bitcast(F32),
                                                 op0=ALU.add, op1=ALU.subtract).then_inc(s_qlo, 1)

                def k_high(it, p):
                    dve.wait_ge(s_k, it * HP + p + 1)
                    if p >= 1:
                        dve.wait_ge(s_klo, (it * HP + p) * 4)
                    dve.tensor_tensor(k_sum[:], psB[:], kr_feat[:, p, :], ALU.add).then_inc(s_ksum, 1)
                    dve.wait_ge(s_ksum, it * HP + p + 1)
                    for a, r in enumerate(halves):
                        dve.tensor_copy(k_hi[r, p % 2, a, :], k_sum[r, :]).then_inc(s_khi, 1)

                def least(it, j):
                    w, a = j // 8, j % 8 // T
                    score_turns.wait()
                    dve.tensor_tensor_reduce(prob[:, j % N_PROB, :], psS[j % 3][:],
                                             kr_bias[:, 2 * w + a, :], -SCALE, 3e38, ALU.add, ALU.min,
                                             neg_max[:, j % N_PROB:j % N_PROB + 1]).then_inc(s_max, 1)

                def copy_odd(it, j):
                    w, a, t = j // 8, j % 8 // T, j % T
                    dve.wait_ge(s_T, it * NT + j + 1)
                    dve.tensor_copy(prob_t[:, w % 2, a, :, t * P:(t + 1) * P],
                                    psT[1].rearrange("p (c q) -> p c q", c=T)).then_inc(s_cv, 1)

                def reciprocals(it, p):
                    dve.wait_ge(s_exp, it * NT + 8 * p + 8)
                    dve.wait_ge(s_wide, it * HP + p + 1)
                    dve.reciprocal(rec[:], sums[:, p % 2, :]).then_inc(s_rec, 1)

                def normalise(it, w):
                    dve.wait_ge(s_rc, it * HP + w + 2)
                    dve.wait_ge(s_pv, it * HP + w + 2)
                    dve.tensor_tensor(attn[:, (w - 1) % HP, :], psV[:], rec_row[:], ALU.mult)\
                       .then_inc(s_attn, 1)

                def add_residual(it, slot):
                    dve.wait_ge(s_done, it + 1)
                    dve.wait_ge(s_res, it + 1)
                    dve.wait_ge(s_o, it + 1)
                    dve.tensor_tensor(y[:], psV[:].rearrange("p (t d) -> p t d", t=T),
                                      h_tok[:, bass.ts(slot, T), :], ALU.add).then_inc(s_y1, 1)

                def add_b_ff2(it):
                    dve.wait_ge(s_f2, it + 1)
                    dve.tensor_tensor(y[:], psA[:].rearrange("p (t d) -> p t d", t=T),
                                      over_tiles(rows[:, 4, :], T), ALU.add).then_inc(s_y2, 1)

                def statistics(it, s_y):
                    stat = small[0]
                    dve.wait_ge(s_y, it + 1)
                    for t in range(T):
                        dve.bn_stats(stat[:, t, :], y[:, t, :]).then_inc(s_stat, 1)

                def variances(ch, stats=stats):
                    stat, mv, rstd = small[0:3]
                    stats.wait()
                    for t in range(T):
                        ch.step(dve.bn_aggr(mv[:, t, :], stat[:, t, :]))
                    ch.wait()
                    dve.tensor_scalar(rstd[:], mv[:, :, 1], EPS, None, ALU.add).then_inc(s_var, 1)

                def rows_out(rstd_turns):
                    rstd_turns.wait()
                    for t in range(T):
                        dve.tensor_scalar(y[:, t, :], y[:, t, :], small[1][:, t, 0:1], small[2][:, t:t + 1],
                                          ALU.subtract, ALU.mult).then_inc(s_norm, 1)

                with dve.Fori(0, L) as l:
                    for h in range(H):
                        dve.wait_ge(s_bias, l * H + h + 1)
                        dve.tensor_copy(kr_bias[:, h, :], (psS2, psS0)[h % 2][:]).then_inc(s_biasc, 1)
                    with dve.Fori(0, B) as b:
                        it = l * B + b
                        ch = Chain(dve, s_ch, it * 2 * T)
                        dve.wait_ge(s_w, tail_weights(it))
                        k_high(it, 0)
                        q_low(it, 0)
                        for j in range(AHEAD):
                            least(it, j)
                        normalise(it, 0)
                        for j in range(NT):
                            w, s = j // 8, j % 8
                            if j + AHEAD < NT:
                                least(it, j + AHEAD)
                            if j % 2 == 1:
                                copy_odd(it, j)
                            if s == 1 and w + 1 < HP:
                                k_high(it, w + 1)
                            if s == 3 and w + 1 < HP:
                                q_low(it, w + 1)
                            if (w, s) == (0, 6):
                                add_residual(it, dve.snap(prev, min_val=0, max_val=B))
                            if (w, s) == (5, 7):
                                add_b_ff2(it)
                                normalise(it, w)
                            if s == 2 and w in (1, 6):
                                statistics(it, s_y1 if w == 1 else s_y2)
                            if s == 4 and w in (1, 6):
                                variances(ch)
                            if s == 6 and w in (1, 6):
                                rows_out(rstd_turns)
                            if s == 5 and w >= 1 and w != 5:
                                normalise(it, w)
                            if (w, s) == (7, 2):
                                dve.wait_ge(s_xhi, it + 2)
                                dve.tensor_tensor(x_lo[:], h_feat[:, (b + 1) % B, :], x_hi[:].bitcast(F32),
                                                  ALU.subtract).then_inc(s_xlo, 1)
                            if s == 7:
                                reciprocals(it, w)
                        dve.reg_mov(prev, b)
                        assert ch.n == 2 * T
                it = L * B
                ch = Chain(dve, s_ch, it * 2 * T)
                last_stats = Counted(dve, s_stat, T, 2 * T * it)
                normalise(it, 0)
                add_residual(it, B - 1)
                last_rstd = Counted(dve, s_rstd, 1, 2 * it)
                statistics(it, s_y1)
                variances(ch, last_stats)
                rows_out(last_rstd)
                add_b_ff2(it)
                statistics(it, s_y2)
                variances(ch, last_stats)
                rows_out(last_rstd)

            @block.tensor
            def _(pe):
                pe.wait_ge(s_const, 48)
                pe.wait_ge(s_uv, 2)
                pe.wait_ge(s_zero, 3)
                pe.sem_inc(s_pv, 1)

                def project_q(it, p):
                    c = slice(p * P, (p + 1) * P)
                    three_pass(pe, psA[:], qk_hi[:, c], qk_lo[:, c], x_hi[:], x_lo[:]).then_inc(s_q, 1)

                def project_k(it, p):
                    c = slice(H * DH + p * P, H * DH + (p + 1) * P)
                    three_pass(pe, psB[:], qk_hi[:, c], qk_lo[:, c], x_hi[:], x_lo[:]).then_inc(s_k, 1)

                def project_v(n, ps):
                    t, c = slice(n % T * P, (n % T + 1) * P), slice(n // T * 4 * P, (n // T + 1) * 4 * P)
                    three_pass(pe, ps[:], x_hi[:, t], x_lo[:, t], vw_hi[:, c], vw_lo[:, c]).then_inc(s_v, 1)

                def scores(it, j):
                    w, a, t = j // 8, j % 8 // T, j % T
                    if j % T == 0:
                        pe.wait_ge(s_qlo, (it * HP + w) * 2 + a + 1)
                        pe.wait_ge(s_kdup, (it * HP + w) * 2 + a + 1)
                        pe.wait_ge(s_klo, (it * HP + w) * 4 + 2 * a + 2)
                    if j >= 3:
                        pe.wait_ge(s_max, it * NT + j - 2)
                    q = q_st[:, w % 2, a, t * P:(t + 1) * P]
                    pe.matmul(psS[j % 3][:], q, k_hi[:, w % 2, a, :], start=True, stop=False)
                    pe.matmul(psS[j % 3][:], q, k_lo[:, w % 2, a, :], start=False, stop=True)\
                        .then_inc(s_S, 1)

                def transposes(it, j):
                    pe.wait_ge(s_exp, it * NT + j + 1)
                    if j >= 2:
                        pe.wait_ge((s_ca, s_cv)[j % 2], it * (NT // 2) + j // 2 + 1)
                    for n in range(T):
                        mm = pe.transpose(psT[j % 2][:, n * P:(n + 1) * P],
                                          prob[:, j % N_PROB, n * P:(n + 1) * P], ident[:])
                    mm.then_inc(s_T, 1)

                def prob_v(it, w, n):
                    p = (w - 1) % HP
                    if n == 0:
                        pe.wait_ge(s_ca, it * (NT // 2) + 4 * w + 1)
                        pe.wait_ge(s_cv, it * (NT // 2) + 4 * w + 1)
                        if w == 1:
                            pe.wait_ge(s_y1, it + 1)
                        else:
                            pe.wait_ge(s_attn, it * HP + w + 1)
                    for a, r in enumerate(halves):
                        c = slice(p % 4 * P + a * DH, p % 4 * P + (a + 1) * DH)
                        mm = pe.matmul(psV[r, :], v_tok[:, n, c], prob_t[:, p % 2, a, n, :],
                                       start=(n == 0), stop=(n == T - 1))
                    if n == T - 1:
                        mm.then_inc(s_pv, 1)

                def spread_rec(it, w, last=False):
                    pe.wait_ge(s_wide, it * HP + w + 1)
                    if w + 1 < HP and not last:
                        pe.wait_ge(s_ksum, it * HP + (w + 2 if w >= 1 else 1))
                    else:
                        pe.wait_ge(s_rc, it * HP + w + 1)
                    for t in range(T):
                        mm = pe.transpose(psB[:, t * P:(t + 1) * P],
                                          rec_wide[:, t].rearrange("p a d -> p (a d)"), ident[:])
                    mm.then_inc(s_r, 1)

                def project_out(it, t):
                    if t == 0:
                        pe.wait_ge(s_attn, it * HP + 2)
                    for p in range(HP):
                        mm = pe.matmul(psV[:, t * P:(t + 1) * P], attn[:, p, t * P:(t + 1) * P],
                                       o_w[:, p, :], start=(p == 0), stop=(p == HP - 1))
                    if t == T - 1:
                        mm.then_inc(s_o, 1)

                def turn_y(it, ready, done):
                    pe.wait_ge(ready, it + 1)
                    for t in range(T):
                        mm = pe.transpose(psA[:, t * P:(t + 1) * P], y[:, t, :], ident[:])
                    mm.then_inc(done, 1)

                def ff1(it, f):
                    pe.matmul((psA, psB)[f % 2][:], f1_w[:, f * P:(f + 1) * P], z_feat[:], start=True,
                              stop=True).then_inc(s_f1, 1)

                def ff2(it, t):
                    for f in range(FB):
                        mm = pe.matmul(psA[:, t * P:(t + 1) * P], ff[:, f, t * P:(t + 1) * P],
                                       f2_w[:, f, :], start=(f == 0), stop=(f == FB - 1))
                    if t == T - 1:
                        mm.then_inc(s_f2, 1)

                with pe.Fori(0, L) as l:
                    pe.wait_ge(s_rin, (l + 1) * 16)
                    for p in range(HP):
                        if p >= 2:
                            pe.wait_ge(s_krc, l * HP + p - 1)
                        pe.matmul(psS[p % 2][:], r_raw[:, p * P:(p + 1) * P], pos[:], start=True,
                                  stop=True).then_inc(s_kr, 1)
                    for h in range(H):
                        pe.wait_ge(s_krc, l * HP + max(h // 2 + 1, HP - 1))
                        if h >= 2:
                            pe.wait_ge(s_biasc, l * H + h)
                        pe.matmul((psS2, psS0)[h % 2][:], vu_pad[:, h:h + 1].to_broadcast([P, P]),
                                  kr_feat[:, h // 2, :], start=True, stop=True).then_inc(s_bias, 1)
                    with pe.Fori(0, B) as b:
                        it = l * B + b
                        pe.wait_ge(s_biasc, (l + 1) * H + 1)
                        pe.wait_ge(s_split, (l + 1) * 2)
                        pe.wait_ge(s_w, tail_weights(it))
                        pe.wait_ge(s_xlo, it + 1)
                        pe.wait_ge(s_done, it + 1)
                        pe.wait_ge(s_rc, it * HP + 1)
                        project_k(it, 0)
                        project_q(it, 0)
                        for n in range(T):
                            prob_v(it, 0, n)
                        for n in range(T):
                            if n == 2:
                                pe.wait_ge(s_qlo, it * HP * 2 + 2)
                            project_v(n, v_bank[n])
                        spread_rec(it, 0)
                        for j in range(AHEAD):
                            if j == 2:
                                pe.wait_ge(s_vc, it * 2 * T + T)
                            scores(it, j)
                        for j in range(NT):
                            w, s = j // 8, j % 8
                            if j + AHEAD < NT:
                                scores(it, j + AHEAD)
                            transposes(it, j)
                            if s == 0 and w + 1 < HP:
                                pe.wait_ge(s_rc, it * HP + max(w, 1) + 1)
                                if w in (3, 4):
                                    pe.wait_ge(s_f1c, it * FB + 2 * w - 4)
                                if w == 5:
                                    pe.wait_ge(s_vc, it * 2 * T + 6)
                                project_k(it, w + 1)
                            if s == 1 and w + 1 < HP:
                                if w in (3, 4):
                                    pe.wait_ge(s_f1c, it * FB + 2 * w - 5)
                                if w == 5:
                                    pe.wait_ge(s_vc, (it + 1) * 2 * T)
                                if w == 6:
                                    pe.wait_ge(s_y2, it + 1)
                                project_q(it, w + 1)
                            if w == 0 and 3 <= s < 7:
                                project_out(it, s - 3)
                            if w >= 1 and 2 <= s < 6:
                                prob_v(it, w, s - 2)
                            if s == 4 and w >= 1:
                                spread_rec(it, w)
                            if (w, s) == (2, 4):
                                pe.wait_ge(s_qlo, (it * HP + 4) * 2)
                                turn_y(it, s_z, s_zt)
                            for f in ff1_at.get((w, s), ()):
                                if f == 0:
                                    pe.wait_ge(s_zc, it + 1)
                                elif f == 2:
                                    pe.wait_ge(s_qlo, (it * HP + 5) * 2)
                                else:
                                    pe.wait_ge(s_rc, it * HP + w + 2)
                                ff1(it, f)
                            for n in v_at.get((w, s), ()):
                                if n == 4:
                                    pe.wait_ge(s_qlo, (it * HP + 6) * 2)
                                elif n == 5:
                                    pe.wait_ge(s_rc, it * HP + 6)
                                else:
                                    pe.wait_ge(s_vc, it * 2 * T + (5 if n == 6 else 7))
                                project_v(n, v_bank[n])
                            if w == 5 and s >= 4:
                                if s == 4:
                                    pe.wait_ge(s_qlo, (it * HP + 7) * 2)
                                    pe.wait_ge(s_f1c, (it + 1) * FB)
                                ff2(it, s - 4)
                            if (w, s) == (7, 5):
                                turn_y(it, s_hn, s_ht)
                it = L * B
                for n in range(T):
                    prob_v(it, 0, n)
                spread_rec(it, 0, last=True)
                for t in range(T):
                    project_out(it, t)
                turn_y(it, s_z, s_zt)
                pe.wait_ge(s_zc, it + 1)
                for f in range(FB):
                    if f >= 2:
                        pe.wait_ge(s_f1c, it * FB + f - 1)
                    ff1(it, f)
                pe.wait_ge(s_f1c, (it + 1) * FB)
                for t in range(T):
                    ff2(it, t)


def experts(nc, ctx, sem, sb_in, bank, ident, h_tok, silu_c, small,
            x, wmod, w1, b1, w2, b2, gate_w, shared_w, shared_b, gamma, beta, out):
    N = B * T
    with ExitStack() as own:
        def sb(name, shape, dt=F32):
            return sb_in(own, name, shape, dt)

        x2 = sb("x2", [P, N, D])
        wm = sb("wm", [P, 4 * D])
        mod = sb("mod", [P, B, 4, D])
        w1_raw = sb("w1_raw", [P, E, DF])
        w2_all = sb("w2_all", [P, E, FB, D])
        b1_all = sb("b1_all", [P, E, FB])
        b2_all = sb("b2_all", [E, D])
        w1_hi = [sb(f"w1_hi{i}", [P, DF], F32R) for i in range(2)]
        w1_lo = [sb(f"w1_lo{i}", [P, DF], F32R) for i in range(2)]
        wg = sb("wg", [P, E])
        ws = sb("ws", [P, D])
        rows3 = sb("rows3", [P, 3, D])
        hm = sb("hm", [P, T, D])
        m_feat = sb("m_feat", [P, S])
        m_hi = sb("m_hi", [P, B * S], F32R)
        m_lo = sb("m_lo", [P, B * S], F32R)
        logit = sb("logit", [P, N, E])
        gsh = sb("gsh", [P, N, D])
        acc = sb("acc", [P, N, D])
        inner = sb("inner", [P, 2, FB, S])
        idx = sb("idx", [P, E])
        pr = sb("pr", [P, N, E])
        top = sb("top", [P, 3, N])
        eq = sb("eq", [P, N, E])
        first = sb("first", [P, N])
        one = sb("one", [P, 2, N, E])
        comb = sb("comb", [P, N, E])
        comb_t = sb("comb_t", [E, N, P])

        s_in, s_iota, s_mod, s_modc = sem("m_in"), sem("m_iota"), sem("m_mod"), sem("m_modc")
        s_ch, s_h, s_tr, s_fe, s_hi, s_lo = (sem("m_ch"), sem("m_h"), sem("m_tr"), sem("m_fe"),
                                             sem("m_hi"), sem("m_lo"))
        s_gate, s_gatec, s_lg, s_e, s_cb, s_ct, s_ctc = (sem("m_gate"), sem("m_gatec"), sem("m_lg"),
                                                         sem("m_e"), sem("m_cb"), sem("m_ct"), sem("m_ctc"))
        s_gelu, s_b2, s_acc = sem("m_gelu"), sem("m_b2"), sem("m_acc")
        s_whi, s_wlo, s_u, s_g, s_y, s_a = (sem("m_whi"), sem("m_wlo"), sem("m_u"), sem("m_g"),
                                            sem("m_y"), sem("m_a"))
        s_out, s_fin = sem("m_out"), sem("m_fin")
        N_IN = 14

        with nc.Block() as block:
            @block.sync
            def _(sp):
                sp.dma_start(wm[:], wmod[:, 2 * D:]).then_inc(s_in, 16)
                sp.dma_start(x2[:], x.rearrange("b (t p) d -> p (b t) d", p=P)).then_inc(s_in, 16)
                sp.dma_start(wg[:], gate_w).then_inc(s_in, 16)
                sp.dma_start(ws[:], shared_w).then_inc(s_in, 16)
                for i, vec in enumerate((shared_b, gamma, beta)):
                    sp.dma_start(rows3[:, i, :], vec.unsqueeze(0).to_broadcast([P, D])).then_inc(s_in, 16)
                sp.dma_start(w1_raw[:], w1.rearrange("e d h -> d e h")).then_inc(s_in, 16)
                for f in range(FB):
                    sp.dma_start(w2_all[:, :, f, :], w2[:, f * P:(f + 1) * P, :].rearrange("e k n -> k e n"))\
                      .then_inc(s_in, 16)
                sp.dma_start(b1_all[:].rearrange("k e f -> k (e f)"),
                             b1.rearrange("e (f k) -> k (e f)", k=P)).then_inc(s_in, 16)
                sp.dma_start(b2_all[:], b2).then_inc(s_in, 16)
                sp.wait_ge(s_fin, B)
                sp.dma_start(out.rearrange("b (t p) d -> p (b t) d", p=P), acc[:]).then_inc(s_out, 16)
                sp.wait_ge(s_out, 16)

            @block.gpsimd
            def _(pool):
                pool.iota(idx[:], pattern=[[1, E]], base=0, channel_multiplier=0,
                          allow_small_or_imprecise_dtypes=True).then_inc(s_iota, 1)
                for n in range(2 * B):
                    inverse_root(pool, small, n + 1)

            @block.scalar
            def _(act):
                for b in range(B):
                    act.wait_ge(s_mod, b + 1)
                    act.activation(mod[:, b].rearrange("p v d -> p (v d)"), bank[b % 2][:], ACT.Copy)\
                       .then_inc(s_modc, 1)
                for b in range(B):
                    act.wait_ge(s_tr, b + 1)
                    act.activation(m_feat[:], bank[2 + b % 2][:], ACT.Copy).then_inc(s_fe, 1)
                    act.activation(m_hi[:, b * S:(b + 1) * S], bank[2 + b % 2][:], ACT.Copy).then_inc(s_hi, 1)
                    act.wait_ge(s_gate, b + 1)
                act.wait_ge(s_lg, 1)
                act.activation(pr[:], logit[:], ACT.Exp).then_inc(s_e, 1)
                act.wait_ge(s_gatec, B)
                act.activation(gsh[:], gsh[:], ACT.Gelu).then_inc(s_gelu, 1)
                up_turns = Turns(act, s_u)
                act.sem_inc(s_g, 1)
                with act.Fori(0, E // 2) as pair:
                    e0 = pair * 2
                    for k in range(2):
                        e = e0 + k
                        if k == 0:
                            act.wait_ge(s_y, e0 * B + 1)
                            for i in range(2):
                                act.activation(w1_hi[i][:], w1_raw[:, e0 + i, :], ACT.Copy).then_inc(s_whi, 1)
                        for g in range(B):
                            for f in range(FB):
                                n = g * FB + f
                                up_turns.wait()
                                act.activation(inner[:, g % 2, f, :], bank[n % 4][:], ACT.Gelu,
                                               bias=b1_all[:, e, f:f + 1]).then_inc(s_g, 1)

            @block.vector
            def _(dve):
                ch, stats = Chain(dve, s_ch), Counted(dve, small[4], T)
                dve.wait_ge(s_in, 16 * N_IN)
                for b in range(B):
                    r = slice(b * T, (b + 1) * T)
                    dve.wait_ge(s_modc, b + 1)
                    for i in (0, 3):
                        ch.link(dve.tensor_scalar(hm[:, i % 2, :], mod[:, b, i, :], 0.0, 2.0, ALU.is_ge,
                                                  ALU.mult))
                        ch.link(dve.scalar_tensor_tensor(out=mod[:, b, i, :], in0=mod[:, b, i, :], scalar=-1.0,
                                                         in1=mod[:, b, i, :], op0=ALU.mult, op1=ALU.max))
                        ch.link(dve.tensor_scalar(mod[:, b, i, :], mod[:, b, i, :], 0.25, None, ALU.max))
                        ch.link(dve.scalar_tensor_tensor(out=mod[:, b, i, :], in0=hm[:, i % 2, :], scalar=-1.0,
                                                         in1=mod[:, b, i, :], op0=ALU.add, op1=ALU.mult))
                    ch.link(dve.tensor_scalar(mod[:, b, 2, :], mod[:, b, 2, :], 1.0, None, ALU.add))
                    ch.link(dve.tensor_tensor(h_tok[:, r, :], h_tok[:, r, :], over_tiles(mod[:, b, 0, :], T),
                                              ALU.mult))
                    ch.link(dve.tensor_tensor(x2[:, r, :], x2[:, r, :], h_tok[:, r, :], ALU.add))
                    if b >= 1:
                        dve.wait_ge(s_tr, b)
                    layer_norm_rows(dve, ch, stats, x2[:, r, :], small, b + 1, hm)
                    ch.link(dve.tensor_tensor(hm[:], hm[:], over_tiles(mod[:, b, 2, :], T), ALU.mult))
                    dve.tensor_tensor(hm[:], hm[:], over_tiles(mod[:, b, 1, :], T), ALU.add).then_inc(s_h, 1)
                    dve.wait_ge(s_hi, b + 1)
                    dve.tensor_tensor(m_lo[:, b * S:(b + 1) * S], bank[2 + b % 2][:],
                                      m_hi[:, b * S:(b + 1) * S].bitcast(F32), ALU.subtract).then_inc(s_lo, 1)
                    dve.wait_ge(s_gate, b + 1)
                    ch.step(dve.tensor_copy(logit[:, r, :],
                                            bank[4][:, 0:T * E].rearrange("p (t e) -> p t e", t=T)))
                    dve.tensor_tensor(gsh[:, r, :], bank[5][:].rearrange("p (t d) -> p t d", t=T),
                                      over_tiles(rows3[:, 0, :], T), ALU.add).then_inc(s_gatec, 1)

                def wide(a):
                    return a.unsqueeze(2).to_broadcast([P, N, E])

                idxs = idx[:].unsqueeze(1).to_broadcast([P, N, E])
                ch.wait()
                ch.link(dve.tensor_reduce(top[:, 0, :], logit[:], AX.X, ALU.max))
                dve.tensor_tensor(logit[:], logit[:], wide(top[:, 0, :]), ALU.subtract).then_inc(s_lg, 1)
                dve.wait_ge(s_e, 1)
                ch.link(dve.tensor_reduce(top[:, 2, :], pr[:], AX.X, ALU.add))
                ch.link(dve.reciprocal(top[:, 2, :], top[:, 2, :]))
                ch.link(dve.tensor_tensor(pr[:], pr[:], wide(top[:, 2, :]), ALU.mult))
                dve.wait_ge(s_iota, 1)
                for k in range(2):
                    ch.link(dve.tensor_reduce(top[:, k, :], pr[:], AX.X, ALU.max))
                    ch.link(dve.tensor_tensor(eq[:], pr[:], wide(top[:, k, :]), ALU.is_equal))
                    ch.link(dve.tensor_scalar(eq[:], eq[:], -float(E), float(E), ALU.mult, ALU.add))
                    ch.link(dve.tensor_tensor(eq[:], eq[:], idxs, ALU.add))
                    ch.link(dve.tensor_reduce(first[:], eq[:], AX.X, ALU.min))
                    ch.link(dve.tensor_tensor(one[:, k], idxs, wide(first[:]), ALU.is_equal))
                    if k == 0:
                        ch.link(dve.scalar_tensor_tensor(out=pr[:], in0=one[:, 0], scalar=-2.0, in1=pr[:],
                                                         op0=ALU.mult, op1=ALU.add))
                ch.link(dve.tensor_tensor(top[:, 2, :], top[:, 0, :], top[:, 1, :], ALU.add))
                ch.link(dve.reciprocal(top[:, 2, :], top[:, 2, :]))
                for k in range(2):
                    ch.link(dve.tensor_tensor(top[:, k, :], top[:, k, :], top[:, 2, :], ALU.mult))
                    ch.link(dve.tensor_tensor(one[:, k], one[:, k], wide(top[:, k, :]), ALU.mult))
                dve.tensor_tensor(comb[:], one[:, 0], one[:, 1], ALU.add).then_inc(s_cb, 1)
                for g in range(B):
                    dve.wait_ge(s_ct, g + 1)
                    dve.tensor_copy(comb_t[:, g * T:(g + 1) * T, :],
                                    bank[6][0:E, :].rearrange("e (t p) -> e t p", t=T)).then_inc(s_ctc, 1)
                dve.wait_ge(s_gelu, 1)
                for g in range(B):
                    dve.wait_ge(s_b2, g + 1)
                    dve.scalar_tensor_tensor(out=acc[:, g * T:(g + 1) * T, :], in0=gsh[:, g * T:(g + 1) * T, :],
                                             scalar=0.5, in1=bank[7][:].rearrange("p (t d) -> p t d", t=T),
                                             op0=ALU.mult, op1=ALU.add).then_inc(s_acc, 1)
                dve.wait_ge(s_acc, B)
                dve.sem_inc(s_a, 1)
                with dve.Fori(0, E // 2) as pair:
                    e0 = pair * 2
                    for k in range(2):
                        e = e0 + k
                        if k == 0:
                            dve.wait_ge(s_whi, e0 + 2)
                            for i in range(2):
                                dve.tensor_tensor(w1_lo[i][:], w1_raw[:, e0 + i, :],
                                                  w1_hi[i][:].bitcast(F32), ALU.subtract).then_inc(s_wlo, 1)
                        for g in range(B):
                            dve.wait_ge(s_y, e * B + g + 2)
                            for t in range(T):
                                n = g * T + t
                                if n == 0:
                                    dve.wait_ge(s_a, e * N + 1)
                                dve.scalar_tensor_tensor(
                                    out=acc[:, n, :], in0=bank[4 + g % 2][:, t * P:(t + 1) * P],
                                    scalar=comb[:, n, bass.ds(e, 1)], in1=acc[:, n, :],
                                    op0=ALU.mult, op1=ALU.add).then_inc(s_a, 1)
                dve.wait_ge(s_a, E * N + 1)
                for b in range(B):
                    r = slice(b * T, (b + 1) * T)
                    rows = acc[:, r, :]
                    layer_norm_rows(dve, ch, stats, rows, small, B + b + 1, rows)
                    ch.link(dve.tensor_tensor(rows, rows, over_tiles(rows3[:, 1, :], T), ALU.mult))
                    ch.link(dve.tensor_tensor(rows, rows, over_tiles(rows3[:, 2, :], T), ALU.add))
                    ch.link(dve.tensor_tensor(rows, rows, over_tiles(mod[:, b, 3, :], T), ALU.mult))
                    dve.tensor_tensor(rows, rows, x2[:, r, :], ALU.add).then_inc(s_fin, 1)

            @block.tensor
            def _(pe):
                pe.wait_ge(s_in, 16 * N_IN)
                for b in range(B):
                    if b >= 2:
                        pe.wait_ge(s_modc, b - 1)
                    pe.matmul(bank[b % 2][:], silu_c[:, b:b + 1].to_broadcast([P, P]), wm[:],
                              start=True, stop=True).then_inc(s_mod, 1)
                for b in range(B):
                    pe.wait_ge(s_h, b + 1)
                    for t in range(T):
                        mm = pe.transpose(bank[2 + b % 2][:, t * P:(t + 1) * P], hm[:, t, :], ident[:])
                    mm.then_inc(s_tr, 1)
                    pe.wait_ge(s_fe, b + 1)
                    if b >= 1:
                        pe.wait_ge(s_gatec, b)
                    for t in range(T):
                        pe.matmul(bank[4][:, t * E:(t + 1) * E], m_feat[:, t * P:(t + 1) * P], wg[:],
                                  start=True, stop=True)
                        mm = pe.matmul(bank[5][:, t * P:(t + 1) * P], m_feat[:, t * P:(t + 1) * P], ws[:],
                                       start=True, stop=True)
                    mm.then_inc(s_gate, 1)
                pe.wait_ge(s_cb, 1)
                for g in range(B):
                    if g >= 1:
                        pe.wait_ge(s_ctc, g)
                    for t in range(T):
                        mm = pe.transpose(bank[6][0:E, t * P:(t + 1) * P], comb[:, g * T + t, :], ident[:])
                    mm.then_inc(s_ct, 1)
                for g in range(B):
                    pe.wait_ge(s_ctc, g + 1)
                    if g >= 1:
                        pe.wait_ge(s_acc, g)
                    for t in range(T):
                        mm = pe.matmul(bank[7][:, t * P:(t + 1) * P], comb_t[:, g * T + t, :], b2_all[:],
                                       start=True, stop=True)
                    mm.then_inc(s_b2, 1)
                pe.wait_ge(s_lo, B)
                pe.sem_inc(s_y, 1)
                with pe.Fori(0, E // 2) as pair:
                    e0 = pair * 2
                    pe.wait_ge(s_wlo, e0 + 2)
                    for k in range(2):
                        e = e0 + k

                        def up(g):
                            for f in range(FB):
                                n = g * FB + f
                                if n >= 4:
                                    pe.wait_ge(s_g, e * B * FB + n - 2)
                                else:
                                    pe.wait_ge(s_g, e * B * FB + 1)
                                w = slice(f * P, (f + 1) * P)
                                m = slice(g * S, (g + 1) * S)
                                pe.matmul(bank[n % 4][:], w1_hi[k][:, w], m_hi[:, m], start=True, stop=False)
                                pe.matmul(bank[n % 4][:], w1_hi[k][:, w], m_lo[:, m], start=False, stop=False)
                                pe.matmul(bank[n % 4][:], w1_lo[k][:, w], m_hi[:, m], start=False, stop=True)\
                                    .then_inc(s_u, 1)

                        def down(g):
                            pe.wait_ge(s_g, e * B * FB + (g + 1) * FB + 1)
                            if g >= 2:
                                pe.wait_ge(s_a, e * N + (g - 1) * T + 1)
                            else:
                                pe.wait_ge(s_a, e * N + 1)
                            for t in range(T):
                                for f in range(FB):
                                    mm = pe.matmul(bank[4 + g % 2][:, t * P:(t + 1) * P],
                                                   inner[:, g % 2, f, t * P:(t + 1) * P],
                                                   w2_all[:, e, f, :], start=(f == 0), stop=(f == FB - 1))
                            mm.then_inc(s_y, 1)

                        up(0)
                        for g in range(B):
                            if g + 1 < B:
                                up(g + 1)
                            down(g)


_INS = ['L0_attn_x', 'L0_attn_W_qkv', 'L0_attn_W_r', 'L0_attn_W_o', 'L0_attn_u', 'L0_attn_v',
        'L0_attn_ln1_g', 'L0_attn_ln1_b', 'L0_attn_W_ff1', 'L0_attn_b_ff1', 'L0_attn_W_ff2',
        'L0_attn_b_ff2', 'L0_attn_ln2_g', 'L0_attn_ln2_b', 'L0_ffn_W1', 'L0_ffn_b1', 'L0_ffn_W2',
        'L0_ffn_b2', 'L0_ffn_gate_W', 'L0_ffn_shared_W', 'L0_ffn_shared_b', 'L0_ffn_gamma',
        'L0_ffn_beta', 'L0_c', 'L0_wmod']


def kernel(**inputs):
    import numpy as _np
    import concourse.bacc as _bacc
    from concourse import mybir as _mybir
    from concourse.bass_utils import run_bass_kernel_spmd as _run

    nc = _bacc.Bacc("TRN2", target_bir_lowering=False, num_devices=1)
    arrays, args = {}, []
    for name in _INS:
        a = _np.ascontiguousarray(inputs[name])
        arrays[f"in_{name}"] = a
        args.append(nc.dram_tensor(f"in_{name}", a.shape, _mybir.dt.from_np(a.dtype),
                                   kind="ExternalInput").ap())
    at = _np.arange(S - 1, -1, -1, dtype=_np.float32)
    freq = (_np.float32(1.0) / _np.float32(10000.0)
            ** (_np.arange(0, D, 2, dtype=_np.float32) / _np.float32(D))).astype(_np.float32)
    ang = freq[:, None] * at[None, :]
    arrays["pos_t"] = _np.concatenate([_np.sin(ang), _np.cos(ang)], axis=0).astype(_np.float32)
    args.append(nc.dram_tensor("pos_t", (D, S), _mybir.dt.float32, kind="ExternalInput").ap())
    args.append(nc.dram_tensor("out_0", (B, S, D), _mybir.dt.float32, kind="ExternalOutput").ap())
    build(nc, *args)
    r = _run(nc, [arrays], core_ids=[0])
    return r.results[0]["out_0"]
```

```python
import concourse.bass as bass
from concourse import mybir
from contextlib import ExitStack

F32 = mybir.dt.float32
F32R = mybir.dt.float32r
ALU = mybir.AluOpType
ACT = mybir.ActivationFunctionType
AX = mybir.AxisListType

P = 128
B = 4
S = 512
D = 128
T = S // P
L = 4
H = 16
DH = 64
HP = H // 2
DF = 512
FB = DF // P
E = 8
NT = HP * 2 * T
EPS = 1e-5
SCALE = DH ** -0.5
N_MOD = 6
SA, CA, GA, SB_, CB, GB = range(N_MOD)


class Turns:

    def __init__(self, eng, sem, start=1, step=1):
        self.eng, self.sem, self.by = eng, sem, step
        self.count = eng.alloc_register(f"turn_{sem.name}")
        eng.reg_mov(self.count, start)

    def wait(self):
        self.eng.wait_ge(self.sem, self.count)
        self.eng.reg_add(self.count, self.count, self.by)


class Counted:

    def __init__(self, eng, sem, step, n=0):
        self.eng, self.sem, self.by, self.n = eng, sem, step, n

    def wait(self):
        self.n += self.by
        self.eng.wait_ge(self.sem, self.n)


class Chain:

    def __init__(self, eng, sem, base=0):
        self.eng, self.sem, self.base, self.n = eng, sem, base, 0

    def step(self, ins):
        self.n += 1
        ins.then_inc(self.sem, 1)

    def wait(self):
        self.eng.wait_ge(self.sem, self.base + self.n)

    def link(self, ins):
        self.step(ins)
        self.wait()


def layer_norm_moments(dve, chain, stats, src, small):
    stat, mv, rstd, _, s_stat, s_var, _ = small
    for t in range(T):
        dve.bn_stats(stat[:, t, :], src[:, t, :]).then_inc(s_stat, 1)
    stats.wait()
    for t in range(T):
        chain.step(dve.bn_aggr(mv[:, t, :], stat[:, t, :]))
    chain.wait()
    dve.tensor_scalar(rstd[:], mv[:, :, 1], EPS, None, ALU.add).then_inc(s_var, 1)


def layer_norm_scale(dve, chain, src, small, count, dst, done=None):
    _, mv, rstd, _, _, _, s_rstd = small
    dve.wait_ge(s_rstd, count)
    for t in range(T):
        ins = dve.tensor_scalar(dst[:, t, :], src[:, t, :], mv[:, t, 0:1], rstd[:, t:t + 1],
                                ALU.subtract, ALU.mult)
        if done is None:
            chain.step(ins)
        else:
            ins.then_inc(done, 1)


def inverse_root(pool, small, count):
    _, _, rstd, exponent, _, s_var, s_rstd = small
    pool.wait_ge(s_var, count)
    pool.tensor_tensor(rstd[:], rstd[:], exponent[:], ALU.pow).then_inc(s_rstd, 1)


def expert_weights(big):
    return big[:, 0:E, :], big[:, E:2 * E, :].rearrange("p e (f n) -> p e f n", f=FB)


def expert_rows(h_tok, h_feat):
    in_tok = h_tok[:, B * T:, :].rearrange("p t d -> p (t d)")
    in_feat = h_feat[:, B, :]
    n = D + E + E * FB
    return (in_tok[:, 0:D + E], in_tok[:, D + E:n].rearrange("p (e f) -> p e f", e=E),
            in_feat[:, 0:3 * D].rearrange("p (i d) -> p i d", i=3), in_feat[0:E, 3 * D:])


def guard(dve, chain, src, sign, size, dst):
    chain.step(dve.tensor_scalar(sign, src, 0.0, 2.0, ALU.is_ge, ALU.mult))
    chain.link(dve.tensor_scalar(size, src, -1.0, None, ALU.mult))
    chain.link(dve.tensor_tensor(size, size, src, ALU.max))
    chain.link(dve.tensor_scalar(size, size, 0.25, None, ALU.max))
    return dve.scalar_tensor_tensor(out=dst, in0=sign, scalar=-1.0, in1=size, op0=ALU.add, op1=ALU.mult)


def over_tiles(row, n):
    return row.unsqueeze(1).to_broadcast([P, n, D])


def build(nc, x, w_qkv, w_r, w_o, u, v, ln1_g, ln1_b, w_ff1, b_ff1, w_ff2, b_ff2, ln2_g, ln2_b,
          w1, b1, w2, b2, gate_w, shared_w, shared_b, gamma, beta, c, wmod, pos_t, out):
    ctx = ExitStack()
    with ctx:
        ctx.enter_context(nc.allow_non_contiguous_dma(reason="small transposed loads of vectors"))

        def sem(name):
            return ctx.enter_context(nc.semaphore(name))

        def sb_in(stack, name, shape, dt=F32):
            return stack.enter_context(nc.sbuf_tensor(name, shape, dt))

        def sb(name, shape, dt=F32):
            return sb_in(ctx, name, shape, dt)

        bank = [ctx.enter_context(nc.psum_tensor(f"bank{i}", [P, 512], F32)) for i in range(8)]

        ident = sb("ident", [P, P])
        h_tok = sb("h_tok", [P, (B + 1) * T, D])
        h_feat = sb("h_feat", [P, B + 1, S])
        silu_c = sb("silu_c", [P, B])
        cols = sb("cols", [P, 2, B])
        exponent = sb("exponent", [P, T])

        def norm_set(i, of=None):
            bufs = of[:4] if of else (sb(f"stat{i}", [P, T, 6]), sb(f"mv{i}", [P, T, 2]),
                                      sb(f"rstd{i}", [P, T]), exponent)
            return bufs + (sem(f"s_stat{i}"), sem(f"s_var{i}"), sem(f"s_rstd{i}"))

        small_in = norm_set(0)
        small = norm_set(1, small_in)
        small_x = norm_set(2)
        sets_in = (small_in, norm_set(3, small_x))
        big = sb("kr_bias", [P, H, S])
        s_xin, s_w1, s_w2, s_small = ([sem(f"x_in{b}") for b in range(B)], sem("m_w1"), sem("m_w2"),
                                      sem("m_small"))

        transformer(nc, ctx, sem, sb_in, bank, ident, h_tok, h_feat, big, silu_c, cols, sets_in, small,
                    small_x, s_xin, s_w1, s_w2, s_small, x, c, wmod, w1, w2, b1, b2, gate_w, shared_w,
                    shared_b, gamma, beta, w_qkv, w_r, w_o, u, v, ln1_g, ln1_b, w_ff1, b_ff1, w_ff2,
                    b_ff2, ln2_g, ln2_b, pos_t)
        experts(nc, ctx, sem, sb_in, bank, ident, h_tok, h_feat, big, silu_c, cols, small_x,
                s_xin, s_w1, s_w2, s_small, wmod, out)


def modulate_in(nc, sem, bank, ident, h_tok, h_feat, silu_c, sets, x, c, wmod, wm, mod,
                early_loads, early_pool):
    with ExitStack() as own:
        c_feat = own.enter_context(nc.sbuf_tensor("c_feat", [P, B], F32))
        s_id, s_c, s_wm = sem("in_ident"), sem("in_c"), sem("in_wm")
        s_x = [sem(f"in_x{b}") for b in range(B)]
        s_exp, s_silu, s_mod, s_modc = sem("in_exp"), sem("in_silu"), sem("in_mod"), sem("in_modc")
        s_chain, s_mul, s_h, s_tr = sem("in_chain"), sem("in_mul"), sem("in_h"), sem("in_tr")
        s_tc, s_ca1 = sem("in_tc"), sem("in_ca1")

        with nc.Block() as block:
            @block.sync
            def _(sp):
                sp.dma_start(c_feat[:], c.rearrange("b d -> d b")).then_inc(s_c, 16)
                sp.dma_start(wm, wmod[:, 0:2 * D]).then_inc(s_wm, 16)
                for b in range(B):
                    sp.dma_start(h_tok[:, b * T:(b + 1) * T, :], x[b].rearrange("(t p) d -> p t d", p=P))\
                      .then_inc(s_x[b], 16)
                early_loads(sp)

            @block.gpsimd
            def _(pool):
                pool.memset(ident[:], 0.0).then_inc(s_id, 1)
                pool.wait_ge(s_id, 1)
                pool.affine_select(out=ident[:], in_=ident[:], compare_op=ALU.not_equal, fill=1.0,
                                   base=0, pattern=[[-1, P]], channel_multiplier=1).then_inc(s_id, 1)
                pool.memset(sets[0][3][:], -0.5).then_inc(s_id, 1)
                pool.wait_ge(s_id, 3)

                def add_sa(b):
                    rows = h_tok[:, b * T:(b + 1) * T, :]
                    pool.wait_ge(s_mul, b + 1)
                    pool.tensor_tensor(rows, rows, over_tiles(mod[:, b, 0:D], T), ALU.add).then_inc(s_h, 1)

                early_pool(pool)
                inverse_root(pool, sets[0], 1)
                for b in range(1, B):
                    inverse_root(pool, sets[b % 2], b // 2 + 1)
                    add_sa(b - 1)
                add_sa(B - 1)

            @block.scalar
            def _(act):
                act.wait_ge(s_c, 16)
                act.activation(silu_c[:], c_feat[:], ACT.Exp, scale=-1.0).then_inc(s_exp, 1)
                for b in range(B):
                    act.wait_ge(s_mod, b + 1)
                    act.activation(mod[:, b, :], bank[b][:, 0:2 * D], ACT.Copy).then_inc(s_modc, 1)
                for b in range(B):
                    act.wait_ge(s_tr, b + 1)
                    act.activation(h_feat[:, b, :], bank[4 + b][:], ACT.Copy).then_inc(s_tc, 1)

            @block.vector
            def _(dve):
                ch, stats = Chain(dve, s_chain), [Counted(dve, n[4], T) for n in sets]
                dve.wait_ge(s_exp, 1)
                ch.link(dve.tensor_scalar(silu_c[:], silu_c[:], 1.0, None, ALU.add))
                ch.link(dve.reciprocal(silu_c[:], silu_c[:]))
                dve.tensor_tensor(silu_c[:], silu_c[:], c_feat[:], ALU.mult).then_inc(s_silu, 1)

                def moments(b):
                    dve.wait_ge(s_x[b], 16)
                    layer_norm_moments(dve, ch, stats[b % 2], h_tok[:, b * T:(b + 1) * T, :], sets[b % 2])

                def rows_out(b):
                    rows = h_tok[:, b * T:(b + 1) * T, :]
                    layer_norm_scale(dve, ch, rows, sets[b % 2], b // 2 + 1, rows)
                    if b == 0:
                        dve.wait_ge(s_modc, B)
                        dve.tensor_scalar(mod[:, :, D:2 * D], mod[:, :, D:2 * D], 1.0, None, ALU.add)\
                           .then_inc(s_ca1, 1)
                        dve.wait_ge(s_ca1, 1)
                    ch.wait()
                    dve.tensor_tensor(rows, rows, over_tiles(mod[:, b, D:2 * D], T), ALU.mult)\
                       .then_inc(s_mul, 1)

                moments(0)
                for b in range(B):
                    if b + 1 < B:
                        moments(b + 1)
                    rows_out(b)

            @block.tensor
            def _(pe):
                pe.wait_ge(s_silu, 1)
                pe.wait_ge(s_wm, 16)
                for b in range(B):
                    pe.matmul(bank[b][:, 0:2 * D], silu_c[:, b:b + 1].to_broadcast([P, P]), wm,
                              start=True, stop=True).then_inc(s_mod, 1)
                pe.wait_ge(s_id, 2)
                for b in range(B):
                    pe.wait_ge(s_h, b + 1)
                    for t in range(T):
                        mm = pe.transpose(bank[4 + b][:, t * P:(t + 1) * P], h_tok[:, b * T + t, :],
                                          ident[:])
                    mm.then_inc(s_tr, 1)


def transformer(nc, ctx, sem, sb_in, bank, ident, h_tok, h_feat, kr_bias, silu_c, cols, sets_in, small,
                small_x, s_xin, s_w1, s_w2, s_small, x, c, wmod, w1, w2, b1, b2, gate_w, shared_w,
                shared_b, gamma, beta, w_qkv, w_r, w_o, u, v, ln1_g, ln1_b, w_ff1, b_ff1, w_ff2,
                b_ff2, ln2_g, ln2_b, pos_t):
    with ExitStack() as own:
        def sb(name, shape, dt=F32):
            return sb_in(own, name, shape, dt)

        qk_hi = sb("qk_hi", [P, 2 * H * DH], F32R)
        qk_lo = sb("qk_lo", [P, 2 * H * DH], F32R)
        vw_hi = sb("vw_hi", [P, H * DH], F32R)
        vw_lo = sb("vw_lo", [P, H * DH], F32R)
        o_w = sb("o_w", [P, HP, D])
        f1_w = sb("f1_w", [P, DF])
        f2_w = sb("f2_w", [P, FB, D])
        rows = sb("rows", [P, 5, D])
        f1_b = sb("f1_b", [P, FB])
        pos = sb("pos", [P, S])
        u_col = sb("u_col", [P, HP])
        vu_pad = sb("vu_pad", [P, H])
        kr_feat = sb("kr_feat", [P, HP, S])
        N_PROB = 4
        AHEAD = 3
        x_hi = sb("x_hi", [P, S], F32R)
        x_lo = sb("x_lo", [P, S], F32R)
        q_st = sb("q_st", [P, 2, 2, S], F32R)
        k_sum = sb("k_sum", [P, S])
        k_hi = sb("k_hi", [P, 2, 2, S], F32R)
        k_lo = sb("k_lo", [P, 2, 2, S], F32R)
        v_tok = sb("v_tok", [P, T, HP // 2 * P])
        neg_max = sb("neg_max", [P, N_PROB])
        sums = sb("sums", [P, 2, 2 * T])
        v_col = sums[:, 0, :]
        rec = sb("rec", [P, 2 * T])
        rec_wide = sb("rec_wide", [P, T, 2, DH])
        rec_row = sb("rec_row", [P, S])
        prob = sb("prob", [P, N_PROB, S])
        prob_t = sb("prob_t", [P, 2, 2, T, S])
        attn = sb("attn", [P, HP, S])
        y = sb("y", [P, T, D])
        z_feat = sb("z_feat", [P, S])
        landing = prob_t[:, 0].rearrange("p a c q -> p (a c q)")
        qk_raw = landing[:, 0:2 * H * DH]
        v_raw = landing[:, 2 * H * DH:3 * H * DH]
        r_raw = kr_feat[:, HP - 2:, :].rearrange("p h s -> p (h s)")
        ff = attn[:, HP // 2:, :]

        (psS0, psS1, psS2, psT0, psT1, psV, psA, psB) = bank
        psS, psT = (psS0, psS1, psS2), (psT0, psT1)
        bias_bank = (psS2, psT0)
        halves = (slice(0, DH), slice(DH, P))
        v_at = {(4, 5): (4,), (4, 6): (5, 6), (4, 7): (7,)}
        v_bank = (psT0, psT1, psA, psS2, psA, psB, psA, psA)
        ff1_at = {(2, 6): (0, 1), (3, 5): (2,), (3, 6): (3,)}

        s_const, s_rin, s_raw, s_w, s_uv, s_zero = (sem("const"), sem("r_in"), sem("raw_in"), sem("w_in"),
                                                    sem("uv"), sem("zero"))
        s_split_hi, s_split = sem("split_hi"), sem("split")
        s_kr, s_bias, s_bias_act, s_bias_dve = sem("kr"), sem("bias"), sem("bias_act"), sem("bias_dve")
        s_krc = (sem("kr_act"), sem("kr_dve"))
        s_xhi, s_xlo = sem("x_hi"), sem("x_lo")
        s_q, s_qhi, s_qlo = sem("q"), sem("q_hi"), sem("q_lo")
        s_k, s_ksum, s_khi, s_kdup, s_klo = sem("k"), sem("k_sum"), sem("k_hi"), sem("k_dup"), sem("k_lo")
        s_v, s_vc = sem("v"), sem("vc")
        s_S, s_max, s_exp = sem("scores"), sem("max"), sem("exp")
        s_T, s_ca, s_cv = sem("probT"), sem("copied_act"), sem("copied_dve")
        s_pv, s_rec, s_wide, s_r, s_rc, s_attn = (sem("pv"), sem("rec"), sem("rec_wide"), sem("r"),
                                                  sem("rc"), sem("attn"))
        s_o, s_y1, s_norm, s_g, s_z, s_zt, s_zc = (sem("o"), sem("y1"), sem("norm"), sem("ln_g"), sem("z"),
                                                   sem("zt"), sem("zc"))
        s_f1, s_f1c, s_f2, s_y2, s_hn, s_ht, s_done, s_res = (
            sem("f1"), sem("f1c"), sem("f2"), sem("y2"), sem("hn"), sem("ht"), sem("done"), sem("res"))
        s_ch = sem("dve_chain")
        N_W = 9
        s_stat, s_var, s_rstd = small[4:7]
        s_wm, s_ga, s_cols = sem("x_wm"), sem("x_ga"), sem("x_cols")
        s_chx = sem("x_chain")
        wm = prob[:, 0, :].rearrange("p (v n) -> p v n", v=4)
        ga = prob[:, 1, :].rearrange("p (b d) -> p b d", b=B)

        def tail_weights(it):
            return ((it + B - 1) // B + 1) * 16 * N_W

        def three_pass(pe, ps, w_hi, w_lo, m_hi, m_lo):
            pe.matmul(ps, w_hi, m_hi, start=True, stop=False)
            pe.matmul(ps, w_hi, m_lo, start=False, stop=False)
            return pe.matmul(ps, w_lo, m_hi, start=False, stop=True)

        def scale_rows(eng, count, g, b_row, done, dst=y[:]):
            eng.wait_ge(s_norm, count * T)
            eng.tensor_tensor(y[:], y[:], over_tiles(rows[:, g, :], T), ALU.mult).then_inc(s_g, 1)
            eng.wait_ge(s_g, count)
            eng.tensor_tensor(dst, y[:], over_tiles(rows[:, b_row, :], T), ALU.add).then_inc(done, 1)

        def load_o(sp, l):
            sp.dma_start(o_w[:], w_o[l].rearrange("(p k) n -> k p n", k=P)).then_inc(s_w, 16)

        def load_f1(sp, l):
            sp.dma_start(f1_w[:], w_ff1[l]).then_inc(s_w, 16)
            sp.dma_start(f1_b[:], b_ff1[l].rearrange("(f k) -> k f", k=P)).then_inc(s_w, 16)

        def load_f2(sp, l):
            sp.dma_start(f2_w[:], w_ff2[l].rearrange("(f k) n -> k f n", k=P)).then_inc(s_w, 16)

        def load_rows(sp, l):
            for i, vec in enumerate((ln1_g, ln1_b, ln2_g, ln2_b, b_ff2)):
                sp.dma_start(rows[:, i, :], vec[l].unsqueeze(0).to_broadcast([P, D]))\
                  .then_inc(s_w, 16)

        def load_r(sp, l):
            sp.dma_start(r_raw, w_r[l]).then_inc(s_rin, 16)

        def load_raw(sp, l):
            sp.dma_start(qk_raw, w_qkv[l, :, 0:2 * H * DH]).then_inc(s_raw, 16)
            sp.dma_start(v_raw, w_qkv[l, :, 2 * H * DH:]).then_inc(s_raw, 16)

        def early_loads(sp):
            sp.dma_start(pos[:], pos_t).then_inc(s_const, 16)
            sp.dma_start(u_col[:], u.rearrange("(p two) d -> (two d) p", two=2)).then_inc(s_const, 16)
            sp.dma_start(v_col[:], v.rearrange("(p two) d -> (two d) p", two=2)).then_inc(s_const, 16)
            load_r(sp, 0)
            load_raw(sp, 0)
            load_o(sp, 0)
            load_f1(sp, 0)
            load_f2(sp, 0)
            load_rows(sp, 0)
        def early_pool(pool):
            for t in (vu_pad[:], v_tok[:], h_tok[:, B * T:, :]):
                pool.memset(t, 0.0).then_inc(s_zero, 1)
            pool.memset(rec_wide[:], 0.0).then_inc(s_wide, 1)

        modulate_in(nc, sem, bank, ident, h_tok, h_feat, silu_c, sets_in, x, c, wmod,
                    prob[:, 2, 0:2 * D], prob[:, 0:2, :].rearrange("p i (j n) -> p (i j) n", j=2),
                    early_loads, early_pool)

        with nc.Block() as block:
            @block.sync
            def _(sp):
                def load_tail(l):
                    it = l * B
                    sp.wait_ge(s_o, it + 1)
                    load_o(sp, l)
                    sp.wait_ge(s_f1c, (it + 1) * FB)
                    load_f1(sp, l)
                    sp.wait_ge(s_f2, it + 1)
                    load_f2(sp, l)
                    sp.wait_ge(s_hn, it + 1)
                    load_rows(sp, l)

                with sp.Fori(0, L - 1) as l:
                    load_tail(l)
                    sp.wait_ge(s_ksum, (l + 1) * B * HP)
                    load_r(sp, l + 1)
                    sp.wait_ge(s_pv, (l + 1) * B * HP + 1)
                    load_raw(sp, l + 1)
                load_tail(L - 1)
                sp.wait_ge(s_T, L * B * NT)
                sp.wait_ge(s_xlo, L * B + 1)
                sp.wait_ge(s_done, L * B + 1)
                sp.dma_start(wm.rearrange("k v n -> k (v n)"), wmod[:, 2 * D:]).then_inc(s_wm, 16)
                for b in range(B):
                    sp.dma_start(h_feat[:, b, :].rearrange("p (t d) -> p t d", t=T),
                                 x[b].rearrange("(t p) d -> p t d", p=P)).then_inc(s_xin[b], 16)
                sp.wait_ge(s_res, 2)
                wsg, b1_all, rows3, b2_all = expert_rows(h_tok, h_feat)
                sp.dma_start(wsg[:, 0:D], shared_w).then_inc(s_small, 16)
                sp.dma_start(wsg[:, D:], gate_w).then_inc(s_small, 16)
                for i, vec in enumerate((shared_b, gamma, beta)):
                    sp.dma_start(rows3[:, i, :], vec.unsqueeze(0).to_broadcast([P, D])).then_inc(s_small, 16)
                sp.dma_start(b1_all.rearrange("k e f -> k (e f)"),
                             b1.rearrange("e (f k) -> k (e f)", k=P)).then_inc(s_small, 16)
                sp.dma_start(b2_all, b2).then_inc(s_small, 16)
                sp.wait_ge(s_max, L * B * NT)
                w1_raw, w2_all = expert_weights(kr_bias)
                sp.dma_start(w1_raw, w1.rearrange("e d h -> d e h")).then_inc(s_w1, 16)
                for f in range(FB):
                    sp.dma_start(w2_all[:, :, f, :], w2[:, f * P:(f + 1) * P, :].rearrange("e k n -> k e n"))\
                      .then_inc(s_w2, 16)

            @block.gpsimd
            def _(pool):
                prev = pool.alloc_register("prev_pool")
                pool.reg_mov(prev, B)
                klo_turns = Turns(pool, s_klo, 4, 4)
                rec_turns, r_turns, hn_turns = Turns(pool, s_rec), Turns(pool, s_r), Turns(pool, s_hn)
                pool.memset(attn[:], 0.0).then_inc(s_cv, 1)
                pool.sem_inc(s_res, 1)

                def k_low(it, p):
                    pool.wait_ge(s_khi, (it * HP + p + 1) * 2)
                    for i in range(4):
                        a, r, to = i // 2, halves[i // 2], halves[(i + 1) // 2 % 2]
                        if i >= 1:
                            pool.wait_ge(s_klo, (it * HP + p) * 4 + i)
                        pool.tensor_tensor(k_lo[to, p % 2, a, :], k_sum[r, :],
                                           k_hi[r, p % 2, a, :].bitcast(F32), ALU.subtract)\
                            .then_inc(s_klo, 1)
                    klo_turns.wait()

                def widen():
                    rec_turns.wait()
                    r_turns.wait()
                    pool.tensor_copy(rec_wide[:], rec[:].rearrange("p (a t) -> p t a", t=T).unsqueeze(3)
                                     .to_broadcast([P, T, 2, DH])).then_inc(s_wide, 1)

                def root(count):
                    pool.wait_ge(s_var, count)
                    pool.tensor_tensor(small[2][:], small[2][:], small[3][:], ALU.pow).then_inc(s_rstd, 1)

                def residual(slot):
                    hn_turns.wait()
                    pool.tensor_copy(h_tok[:, bass.ts(slot, T), :], y[:]).then_inc(s_res, 1)

                with pool.Fori(0, L) as l:
                    for part in range(3):
                        n = H * DH
                        lo, hi = ((qk_lo[:, 0:n], qk_hi[:, 0:n]), (qk_lo[:, n:], qk_hi[:, n:]),
                                  (vw_lo[:], vw_hi[:]))[part]
                        pool.wait_ge(s_split_hi, l * 3 + part + 1)
                        pool.tensor_tensor(lo, landing[:, part * n:(part + 1) * n], hi.bitcast(F32),
                                           ALU.subtract).then_inc(s_split, 1)
                    with pool.Fori(0, B) as b:
                        it = l * B + b
                        pool.wait_ge(s_w, tail_weights(it))
                        k_low(it, 0)
                        for w in range(HP):
                            if w >= 1:
                                widen()
                            if w + 1 < HP:
                                k_low(it, w + 1)
                            if w == 1:
                                root(it * 2 + 1)
                                scale_rows(pool, it * 2 + 1, 0, 1, s_z)
                            if w == 6:
                                root(it * 2 + 2)
                            if w == 7:
                                scale_rows(pool, it * 2 + 2, 2, 3, s_hn)
                                residual(pool.snap(prev, min_val=0, max_val=B))
                        widen()
                        pool.reg_mov(prev, b)
                it = L * B
                inverse_root(pool, small_x, 1)
                root(it * 2 + 1)
                inverse_root(pool, small_x, 2)
                inverse_root(pool, small_x, 3)
                root(it * 2 + 2)

            @block.scalar
            def _(act):
                prev = act.alloc_register("prev_act")
                act.reg_mov(prev, B)
                done_turns, ht_turns = Turns(act, s_done), Turns(act, s_ht)
                act.sem_inc(s_done, 1)
                act.sem_inc(s_rc, 1)
                act.activation(x_hi[:], h_feat[:, 0, :], ACT.Copy).then_inc(s_xhi, 1)

                def q_high(it, p):
                    act.wait_ge(s_q, it * HP + p + 1)
                    for a, r in enumerate(halves):
                        act.activation(q_st[r, p % 2, a, :], psA[r, :], ACT.Identity,
                                       bias=u_col[r, p:p + 1]).then_inc(s_qhi, 1)

                def k_double(it, p):
                    for a, r in enumerate(halves):
                        act.wait_ge(s_khi, (it * HP + p) * 2 + a + 1)
                        act.activation(k_hi[halves[1 - a], p % 2, a, :], k_hi[r, p % 2, a, :].bitcast(F32),
                                       ACT.Copy).then_inc(s_kdup, 1)

                def v_out(it, n, ps):
                    act.wait_ge(s_v, it * 2 * T + n + 1)
                    act.activation(v_tok[:, n % T, :], ps[:], ACT.Copy).then_inc(s_vc, 1)

                def r_out(it, w):
                    act.wait_ge(s_r, it * HP + w + 1)
                    act.wait_ge(s_attn, it * HP + w + 1)
                    act.activation(rec_row[:], psB[:], ACT.Copy).then_inc(s_rc, 1)

                def exponential(it, j):
                    act.wait_ge(s_max, it * NT + j + 1)
                    w = j // 8
                    act.activation(prob[:, j % N_PROB, :], prob[:, j % N_PROB, :], ACT.Exp, scale=-1.0,
                                   bias=neg_max[:, j % N_PROB:j % N_PROB + 1],
                                   accum_out=sums[:, w % 2, j % 8:j % 8 + 1]).then_inc(s_exp, 1)

                def copy_even(it, j):
                    w, a, t = j // 8, j % 8 // T, j % T
                    act.wait_ge(s_T, it * NT + j + 1)
                    act.activation(prob_t[:, w % 2, a, :, t * P:(t + 1) * P],
                                   psT[0].rearrange("p (c q) -> p c q", c=T), ACT.Copy).then_inc(s_ca, 1)

                def z_out(it):
                    act.wait_ge(s_zt, it + 1)
                    act.activation(z_feat[:], psA[:], ACT.Copy).then_inc(s_zc, 1)

                def relu(it, f):
                    act.wait_ge(s_f1, it * FB + f + 1)
                    act.activation(ff[:, f, :], (psA, psB)[f % 2][:], ACT.Relu, bias=f1_b[:, f:f + 1])\
                        .then_inc(s_f1c, 1)

                with act.Fori(0, L) as l:
                    for p in range(HP + 1):
                        if p < HP and p % 2 == 0:
                            act.wait_ge(s_kr, l * HP + (p + 1 if p < HP - 2 else HP))
                            act.activation(kr_feat[:, p, :], psS[p % 2][:], ACT.Copy).then_inc(s_krc[0], 1)
                        if p >= 1:
                            act.wait_ge(s_bias, l * HP + p)
                            for r in halves:
                                act.activation(kr_bias[r, 2 * p - 1, :], bias_bank[(p - 1) % 2][halves[1], :],
                                               ACT.Copy).then_inc(s_bias_act, 1)
                        if p == 3:
                            act.wait_ge(s_raw, (l + 1) * 32)
                        if 3 <= p < 6:
                            part, n = p - 3, H * DH
                            to = (qk_hi[:, 0:n], qk_hi[:, n:], vw_hi[:])[part]
                            act.activation(to, landing[:, part * n:(part + 1) * n], ACT.Copy)\
                                .then_inc(s_split_hi, 1)
                    with act.Fori(0, B) as b:
                        it = l * B + b
                        act.wait_ge(s_w, tail_weights(it))
                        q_high(it, 0)
                        k_double(it, 0)
                        act.wait_ge(s_pv, it * HP + 2)
                        for n in range(T):
                            v_out(it, n, v_bank[n])
                        r_out(it, 0)
                        for j in range(AHEAD):
                            exponential(it, j)
                        for j in range(NT):
                            w, s = j // 8, j % 8
                            if j % 2 == 0:
                                copy_even(it, j)
                            if j + AHEAD < NT:
                                exponential(it, j + AHEAD)
                            if s == 1 and w + 1 < HP:
                                q_high(it, w + 1)
                            if s == 2 and w + 1 < HP:
                                k_double(it, w + 1)
                            if s == 4 and w >= 1:
                                r_out(it, w)
                            if (w, s) == (2, 4):
                                z_out(it)
                            for f in ff1_at.get((w, s), ()):
                                relu(it, f)
                            for n in v_at.get((w, s), ()):
                                act.wait_ge(s_pv, it * HP + 6)
                                v_out(it, n, v_bank[n])
                            if (w, s) == (7, 1):
                                done_turns.wait()
                                act.activation(x_hi[:], h_feat[:, (b + 1) % B, :], ACT.Copy).then_inc(s_xhi, 1)
                            if (w, s) == (7, 6):
                                ht_turns.wait()
                                act.activation(h_feat[:, act.snap(prev, min_val=0, max_val=B), :], psA[:],
                                               ACT.Copy).then_inc(s_done, 1)
                        act.reg_mov(prev, b)
                it = L * B
                r_out(it, 0)
                z_out(it)
                for f in range(FB):
                    relu(it, f)

            @block.vector
            def _(dve):
                prev = dve.alloc_register("prev_dve")
                dve.reg_mov(prev, B)
                score_turns, stats = Turns(dve, s_S), Turns(dve, s_stat, T, T)
                rstd_turns = Turns(dve, s_rstd)
                dve.wait_ge(s_xhi, 1)
                dve.tensor_tensor(x_lo[:], h_feat[:, 0, :], x_hi[:].bitcast(F32), ALU.subtract)\
                    .then_inc(s_xlo, 1)
                dve.wait_ge(s_const, 48)
                dve.wait_ge(s_zero, 3)
                for a, r in enumerate(halves):
                    dve.tensor_tensor(vu_pad[r, a::2], v_col[r, :], u_col[r, :], ALU.subtract)\
                       .then_inc(s_uv, 1)
                dve.memset(prob_t[:, 1], 0.0).then_inc(s_ca, 1)
                dve.sem_inc(s_attn, 1)

                def q_low(it, p):
                    for a, r in enumerate(halves):
                        dve.wait_ge(s_qhi, (it * HP + p) * 2 + a + 1)
                        dve.scalar_tensor_tensor(out=q_st[halves[1 - a], p % 2, a, :], in0=psA[r, :],
                                                 scalar=u_col[r, p:p + 1],
                                                 in1=q_st[r, p % 2, a, :].bitcast(F32),
                                                 op0=ALU.add, op1=ALU.subtract).then_inc(s_qlo, 1)

                def k_high(it, p):
                    dve.wait_ge(s_k, it * HP + p + 1)
                    if p >= 1:
                        dve.wait_ge(s_klo, (it * HP + p) * 4)
                    dve.tensor_tensor(k_sum[:], psB[:], kr_feat[:, p, :], ALU.add).then_inc(s_ksum, 1)
                    dve.wait_ge(s_ksum, it * HP + p + 1)
                    for a, r in enumerate(halves):
                        dve.tensor_copy(k_hi[r, p % 2, a, :], k_sum[r, :]).then_inc(s_khi, 1)

                def least(it, j):
                    w, a = j // 8, j % 8 // T
                    score_turns.wait()
                    dve.tensor_tensor_reduce(prob[:, j % N_PROB, :], psS[j % 3][:],
                                             kr_bias[:, 2 * w + a, :], -SCALE, 3e38, ALU.add, ALU.min,
                                             neg_max[:, j % N_PROB:j % N_PROB + 1]).then_inc(s_max, 1)

                def copy_odd(it, j):
                    w, a, t = j // 8, j % 8 // T, j % T
                    dve.wait_ge(s_T, it * NT + j + 1)
                    dve.tensor_copy(prob_t[:, w % 2, a, :, t * P:(t + 1) * P],
                                    psT[1].rearrange("p (c q) -> p c q", c=T)).then_inc(s_cv, 1)

                def reciprocals(it, p):
                    dve.wait_ge(s_exp, it * NT + 8 * p + 8)
                    dve.wait_ge(s_wide, it * HP + p + 1)
                    dve.reciprocal(rec[:], sums[:, p % 2, :]).then_inc(s_rec, 1)

                def normalise(it, w):
                    dve.wait_ge(s_rc, it * HP + w + 2)
                    dve.wait_ge(s_pv, it * HP + w + 2)
                    dve.tensor_tensor(attn[:, (w - 1) % HP, :], psV[:], rec_row[:], ALU.mult)\
                       .then_inc(s_attn, 1)

                def add_residual(it, slot):
                    dve.wait_ge(s_done, it + 1)
                    dve.wait_ge(s_res, it + 1)
                    dve.wait_ge(s_o, it + 1)
                    dve.tensor_tensor(y[:], psV[:].rearrange("p (t d) -> p t d", t=T),
                                      h_tok[:, bass.ts(slot, T), :], ALU.add).then_inc(s_y1, 1)

                def add_b_ff2(it):
                    dve.wait_ge(s_f2, it + 1)
                    dve.tensor_tensor(y[:], psA[:].rearrange("p (t d) -> p t d", t=T),
                                      over_tiles(rows[:, 4, :], T), ALU.add).then_inc(s_y2, 1)

                def statistics(it, s_y):
                    stat = small[0]
                    dve.wait_ge(s_y, it + 1)
                    for t in range(T):
                        dve.bn_stats(stat[:, t, :], y[:, t, :]).then_inc(s_stat, 1)

                def variances(ch, stats=stats):
                    stat, mv, rstd = small[0:3]
                    stats.wait()
                    for t in range(T):
                        ch.step(dve.bn_aggr(mv[:, t, :], stat[:, t, :]))
                    ch.wait()
                    dve.tensor_scalar(rstd[:], mv[:, :, 1], EPS, None, ALU.add).then_inc(s_var, 1)

                def rows_out(rstd_turns):
                    rstd_turns.wait()
                    for t in range(T):
                        dve.tensor_scalar(y[:, t, :], y[:, t, :], small[1][:, t, 0:1], small[2][:, t:t + 1],
                                          ALU.subtract, ALU.mult).then_inc(s_norm, 1)

                with dve.Fori(0, L) as l:
                    for p in range(HP + 1):
                        if p < HP and p % 2 == 1:
                            dve.wait_ge(s_kr, l * HP + p + 1)
                            dve.tensor_copy(kr_feat[:, p, :], psS[p % 2][:]).then_inc(s_krc[1], 1)
                        if p >= 1:
                            dve.wait_ge(s_bias, l * HP + p)
                            for r in halves:
                                dve.tensor_copy(kr_bias[r, 2 * p - 2, :], bias_bank[(p - 1) % 2][halves[0], :])\
                                    .then_inc(s_bias_dve, 1)
                    with dve.Fori(0, B) as b:
                        it = l * B + b
                        ch = Chain(dve, s_ch, it * 2 * T)
                        dve.wait_ge(s_w, tail_weights(it))
                        k_high(it, 0)
                        q_low(it, 0)
                        for j in range(AHEAD):
                            least(it, j)
                        normalise(it, 0)
                        for j in range(NT):
                            w, s = j // 8, j % 8
                            if j + AHEAD < NT:
                                least(it, j + AHEAD)
                            if j % 2 == 1:
                                copy_odd(it, j)
                            if s == 1 and w + 1 < HP:
                                k_high(it, w + 1)
                            if s == 3 and w + 1 < HP:
                                q_low(it, w + 1)
                            if (w, s) == (0, 6):
                                add_residual(it, dve.snap(prev, min_val=0, max_val=B))
                            if (w, s) == (5, 7):
                                add_b_ff2(it)
                                normalise(it, w)
                            if s == 2 and w in (1, 6):
                                statistics(it, s_y1 if w == 1 else s_y2)
                            if s == 4 and w in (1, 6):
                                variances(ch)
                            if (w, s) in ((1, 6), (7, 2)):
                                rows_out(rstd_turns)
                            if s == 5 and w >= 1 and w != 5:
                                normalise(it, w)
                            if (w, s) == (7, 3):
                                dve.wait_ge(s_xhi, it + 2)
                                dve.tensor_tensor(x_lo[:], h_feat[:, (b + 1) % B, :], x_hi[:].bitcast(F32),
                                                  ALU.subtract).then_inc(s_xlo, 1)
                            if s == 7:
                                reciprocals(it, w)
                        dve.reg_mov(prev, b)
                        assert ch.n == 2 * T
                it = L * B
                ch = Chain(dve, s_ch, it * 2 * T)
                chx, statsx = Chain(dve, s_chx), Counted(dve, small_x[4], T)
                last_stats = Counted(dve, s_stat, T, 2 * T * it)
                last_rstd = Counted(dve, s_rstd, 1, 2 * it)

                def x2_of(b):
                    return h_feat[:, b, :].rearrange("p (t d) -> p t d", t=T)

                def add_x(b):
                    r = slice(b * T, (b + 1) * T)
                    chx.link(dve.tensor_tensor(h_tok[:, r, :], h_tok[:, r, :], over_tiles(ga[:, b, :], T),
                                               ALU.mult))
                    if b < B - 1:
                        dve.wait_ge(s_xin[b], 16)
                        chx.link(dve.tensor_tensor(x2_of(b), x2_of(b), h_tok[:, r, :], ALU.add))
                        layer_norm_moments(dve, chx, statsx, x2_of(b), small_x)

                def x2_rows(b):
                    layer_norm_scale(dve, chx, x2_of(b), small_x, b + 1, h_tok[:, b * T:(b + 1) * T, :])

                normalise(it, 0)
                dve.wait_ge(s_ga, 1)
                dve.tensor_copy(cols[:, 0, :], psS1[:, 0:B]).then_inc(s_cols, 1)
                dve.tensor_scalar(cols[:, 1, :], psS1[:, B:2 * B], 1.0, None, ALU.add).then_inc(s_cols, 1)
                chx.link(guard(dve, chx, psS0[:], prob[:, 2, :], prob[:, 3, :], prob[:, 1, :]))
                dve.wait_ge(s_res, it + 1)
                add_x(0)
                add_residual(it, B - 1)
                statistics(it, s_y1)
                variances(ch, last_stats)
                rows_out(last_rstd)
                scale_rows(dve, it * 2 + 1, 0, 1, s_z)
                x2_rows(0)
                add_x(1)
                x2_rows(1)
                add_x(2)
                x2_rows(2)
                add_b_ff2(it)
                statistics(it, s_y2)
                variances(ch, last_stats)
                rows_out(last_rstd)
                scale_rows(dve, it * 2 + 2, 2, 3, s_hn, h_tok[:, (B - 1) * T:B * T, :])
                dve.wait_ge(s_hn, it + 1)
                add_x(B - 1)

            @block.tensor
            def _(pe):
                pe.wait_ge(s_const, 48)
                pe.wait_ge(s_uv, 2)
                pe.wait_ge(s_zero, 3)
                pe.sem_inc(s_pv, 1)

                def project_q(it, p):
                    c = slice(p * P, (p + 1) * P)
                    three_pass(pe, psA[:], qk_hi[:, c], qk_lo[:, c], x_hi[:], x_lo[:]).then_inc(s_q, 1)

                def project_k(it, p):
                    c = slice(H * DH + p * P, H * DH + (p + 1) * P)
                    three_pass(pe, psB[:], qk_hi[:, c], qk_lo[:, c], x_hi[:], x_lo[:]).then_inc(s_k, 1)

                def project_v(n, ps):
                    t, c = slice(n % T * P, (n % T + 1) * P), slice(n // T * 4 * P, (n // T + 1) * 4 * P)
                    three_pass(pe, ps[:], x_hi[:, t], x_lo[:, t], vw_hi[:, c], vw_lo[:, c]).then_inc(s_v, 1)

                def scores(it, j):
                    w, a, t = j // 8, j % 8 // T, j % T
                    if j % T == 0:
                        pe.wait_ge(s_qlo, (it * HP + w) * 2 + a + 1)
                        pe.wait_ge(s_kdup, (it * HP + w) * 2 + a + 1)
                        pe.wait_ge(s_klo, (it * HP + w) * 4 + 2 * a + 2)
                    if j >= 3:
                        pe.wait_ge(s_max, it * NT + j - 2)
                    q = q_st[:, w % 2, a, t * P:(t + 1) * P]
                    pe.matmul(psS[j % 3][:], q, k_hi[:, w % 2, a, :], start=True, stop=False)
                    pe.matmul(psS[j % 3][:], q, k_lo[:, w % 2, a, :], start=False, stop=True)\
                        .then_inc(s_S, 1)

                def transposes(it, j):
                    pe.wait_ge(s_exp, it * NT + j + 1)
                    if j >= 2:
                        pe.wait_ge((s_ca, s_cv)[j % 2], it * (NT // 2) + j // 2 + 1)
                    for n in range(T):
                        mm = pe.transpose(psT[j % 2][:, n * P:(n + 1) * P],
                                          prob[:, j % N_PROB, n * P:(n + 1) * P], ident[:])
                    mm.then_inc(s_T, 1)

                def prob_v(it, w, n):
                    p = (w - 1) % HP
                    if n == 0:
                        pe.wait_ge(s_ca, it * (NT // 2) + 4 * w + 1)
                        pe.wait_ge(s_cv, it * (NT // 2) + 4 * w + 1)
                        if w == 1:
                            pe.wait_ge(s_y1, it + 1)
                        else:
                            pe.wait_ge(s_attn, it * HP + w + 1)
                    for a, r in enumerate(halves):
                        c = slice(p % 4 * P + a * DH, p % 4 * P + (a + 1) * DH)
                        mm = pe.matmul(psV[r, :], v_tok[:, n, c], prob_t[:, p % 2, a, n, :],
                                       start=(n == 0), stop=(n == T - 1))
                    if n == T - 1:
                        mm.then_inc(s_pv, 1)

                def spread_rec(it, w, last=False):
                    pe.wait_ge(s_wide, it * HP + w + 1)
                    if w + 1 < HP and not last:
                        pe.wait_ge(s_ksum, it * HP + (w + 2 if w >= 1 else 1))
                    else:
                        pe.wait_ge(s_rc, it * HP + w + 1)
                    for t in range(T):
                        mm = pe.transpose(psB[:, t * P:(t + 1) * P],
                                          rec_wide[:, t].rearrange("p a d -> p (a d)"), ident[:])
                    mm.then_inc(s_r, 1)

                def project_out(it, t):
                    if t == 0:
                        pe.wait_ge(s_attn, it * HP + 2)
                    for p in range(HP):
                        mm = pe.matmul(psV[:, t * P:(t + 1) * P], attn[:, p, t * P:(t + 1) * P],
                                       o_w[:, p, :], start=(p == 0), stop=(p == HP - 1))
                    if t == T - 1:
                        mm.then_inc(s_o, 1)

                def turn_y(it, ready, done):
                    pe.wait_ge(ready, it + 1)
                    for t in range(T):
                        mm = pe.transpose(psA[:, t * P:(t + 1) * P], y[:, t, :], ident[:])
                    mm.then_inc(done, 1)

                def ff1(it, f):
                    pe.matmul((psA, psB)[f % 2][:], f1_w[:, f * P:(f + 1) * P], z_feat[:], start=True,
                              stop=True).then_inc(s_f1, 1)

                def ff2(it, t):
                    for f in range(FB):
                        mm = pe.matmul(psA[:, t * P:(t + 1) * P], ff[:, f, t * P:(t + 1) * P],
                                       f2_w[:, f, :], start=(f == 0), stop=(f == FB - 1))
                    if t == T - 1:
                        mm.then_inc(s_f2, 1)

                with pe.Fori(0, L) as l:
                    pe.wait_ge(s_rin, (l + 1) * 16)
                    for p in range(HP + 1):
                        if p < HP:
                            if p >= 2:
                                pe.wait_ge(s_krc[p % 2], l * (HP // 2) + p // 2)
                            pe.matmul(psS[p % 2][:], r_raw[:, p * P:(p + 1) * P], pos[:], start=True,
                                      stop=True).then_inc(s_kr, 1)
                        if p >= 1:
                            pe.wait_ge(s_krc[(p - 1) % 2], l * (HP // 2) + (p - 1) // 2 + 1)
                            if p == 2:
                                pe.wait_ge(s_ca, l * B * (NT // 2) + 1)
                            if p >= 3:
                                pe.wait_ge(s_bias_act, (l * HP + p - 2) * 2)
                                pe.wait_ge(s_bias_dve, (l * HP + p - 2) * 2)
                            for a, r in enumerate(halves):
                                h = 2 * (p - 1) + a
                                mm = pe.matmul(bias_bank[(p - 1) % 2][r, :],
                                               vu_pad[:, h:h + 1].to_broadcast([P, DH]),
                                               kr_feat[:, p - 1, :], start=True, stop=True)
                            mm.then_inc(s_bias, 1)
                    with pe.Fori(0, B) as b:
                        it = l * B + b
                        pe.wait_ge(s_split, (l + 1) * 3)
                        pe.wait_ge(s_w, tail_weights(it))
                        pe.wait_ge(s_xlo, it + 1)
                        pe.wait_ge(s_rc, it * HP + 1)
                        project_k(it, 0)
                        pe.wait_ge(s_done, it + 1)
                        project_q(it, 0)
                        for n in range(T):
                            prob_v(it, 0, n)
                        pe.wait_ge(s_bias_act, (l + 1) * H)
                        pe.wait_ge(s_bias_dve, (l + 1) * H)
                        for n in range(T):
                            if n == 2:
                                pe.wait_ge(s_qlo, it * HP * 2 + 2)
                            project_v(n, v_bank[n])
                        spread_rec(it, 0)
                        for j in range(AHEAD):
                            if j == 2:
                                pe.wait_ge(s_vc, it * 2 * T + T)
                            scores(it, j)
                        for j in range(NT):
                            w, s = j // 8, j % 8
                            if j + AHEAD < NT:
                                scores(it, j + AHEAD)
                            transposes(it, j)
                            if s == 0 and w + 1 < HP:
                                pe.wait_ge(s_rc, it * HP + max(w, 1) + 1)
                                if w in (3, 4):
                                    pe.wait_ge(s_f1c, it * FB + 2 * w - 4)
                                if w == 5:
                                    pe.wait_ge(s_vc, it * 2 * T + 6)
                                project_k(it, w + 1)
                            if s == 1 and w + 1 < HP:
                                if w in (3, 4):
                                    pe.wait_ge(s_f1c, it * FB + 2 * w - 5)
                                if w == 5:
                                    pe.wait_ge(s_vc, (it + 1) * 2 * T)
                                if w == 6:
                                    pe.wait_ge(s_y2, it + 1)
                                project_q(it, w + 1)
                            if w == 0 and 3 <= s < 7:
                                project_out(it, s - 3)
                            if w >= 1 and 2 <= s < 6:
                                prob_v(it, w, s - 2)
                            if s == 4 and w >= 1:
                                spread_rec(it, w)
                            if (w, s) == (2, 4):
                                pe.wait_ge(s_qlo, (it * HP + 4) * 2)
                                turn_y(it, s_z, s_zt)
                            for f in ff1_at.get((w, s), ()):
                                if f == 0:
                                    pe.wait_ge(s_zc, it + 1)
                                elif f == 2:
                                    pe.wait_ge(s_qlo, (it * HP + 5) * 2)
                                else:
                                    pe.wait_ge(s_rc, it * HP + w + 2)
                                ff1(it, f)
                            for n in v_at.get((w, s), ()):
                                if n == 4:
                                    pe.wait_ge(s_qlo, (it * HP + 6) * 2)
                                elif n == 5:
                                    pe.wait_ge(s_rc, it * HP + 6)
                                else:
                                    pe.wait_ge(s_vc, it * 2 * T + (5 if n == 6 else 7))
                                project_v(n, v_bank[n])
                            if w == 5 and s >= 4:
                                if s == 4:
                                    pe.wait_ge(s_qlo, (it * HP + 7) * 2)
                                    pe.wait_ge(s_f1c, (it + 1) * FB)
                                ff2(it, s - 4)
                            if (w, s) == (7, 6):
                                turn_y(it, s_hn, s_ht)
                it = L * B
                for n in range(T):
                    prob_v(it, 0, n)
                spread_rec(it, 0, last=True)
                pe.wait_ge(s_wm, 16)
                for b in range(B):
                    pe.matmul(psS0[:, b * D:(b + 1) * D], silu_c[:, b:b + 1].to_broadcast([P, P]), wm[:, 0, :],
                              start=True, stop=True)
                for i, vec in enumerate((1, 2)):
                    mm = pe.matmul(psS1[:, i * B:(i + 1) * B], wm[:, vec, :], silu_c[:], start=True, stop=True)
                mm.then_inc(s_ga, 1)
                for t in range(T):
                    project_out(it, t)
                turn_y(it, s_z, s_zt)
                pe.wait_ge(s_zc, it + 1)
                for f in range(FB):
                    if f >= 2:
                        pe.wait_ge(s_f1c, it * FB + f - 1)
                    ff1(it, f)
                pe.wait_ge(s_f1c, (it + 1) * FB)
                for t in range(T):
                    ff2(it, t)


def experts(nc, ctx, sem, sb_in, bank, ident, h_tok, h_feat, big, silu_c, cols, small,
            s_xin, s_w1, s_w2, s_small, wmod, out):
    N = B * T
    with ExitStack() as own:
        def sb(name, shape, dt=F32):
            return sb_in(own, name, shape, dt)

        wm = sb("wm", [P, D])
        gb = sb("gb", [P, B, D])
        gtmp = sb("gtmp", [P, 2, B, D])
        w1_raw, w2_all = expert_weights(big)
        wsg, b1_all, rows3, b2_all = expert_rows(h_tok, h_feat)
        w1_hi = [sb(f"w1_hi{i}", [P, DF], F32R) for i in range(2)]
        w1_lo = [sb(f"w1_lo{i}", [P, DF], F32R) for i in range(2)]
        m_feat = sb("m_feat", [P, B * S])
        m_hi = sb("m_hi", [P, B * S], F32R)
        m_lo = sb("m_lo", [P, B * S], F32R)
        logit = sb("logit", [P, N, E])
        gsh = sb("gsh", [P, N, D])
        acc = sb("acc", [P, N, D])
        inner = sb("inner", [P, 2, FB, S])
        idx = sb("idx", [P, E])
        pr = sb("pr", [P, N, E])
        top = sb("top", [P, 3, N])
        eq = sb("eq", [P, N, E])
        first = sb("first", [P, N])
        one = sb("one", [P, 2, N, E])
        comb = sb("comb", [P, N, E])
        comb_t = sb("comb_t", [E, N, P])

        s_wm, s_x2, s_h = sem("m_wm"), sem("m_x2"), sem("m_h")
        s_iota, s_zero, s_mod = sem("m_iota"), sem("m_zero"), sem("m_mod")
        s_ch, s_tr, s_fe, s_hi, s_lo = sem("m_ch"), sem("m_tr"), sem("m_fe"), sem("m_hi"), sem("m_lo")
        s_gate, s_gatec, s_lg, s_e, s_cb, s_ct, s_ctc = (sem("m_gate"), sem("m_gatec"), sem("m_lg"),
                                                         sem("m_e"), sem("m_cb"), sem("m_ct"), sem("m_ctc"))
        s_gelu, s_b2, s_base, s_gb, s_gb2 = (sem("m_gelu"), sem("m_b2"), sem("m_base"), sem("m_gb"),
                                             sem("m_gb2"))
        s_whi, s_wlo, s_u, s_g, s_y, s_a = (sem("m_whi"), sem("m_wlo"), sem("m_u"), sem("m_g"),
                                            sem("m_y"), sem("m_a"))
        s_out, s_fin = sem("m_out"), sem("m_fin")
        N_SMALL = 7
        LAST = E - 2
        AHEAD = 2 * T

        def x2_of(b):
            return h_feat[:, b, :].rearrange("p (t d) -> p t d", t=T)

        with nc.Block() as block:
            @block.sync
            def _(sp):
                sp.dma_start(wm[:], wmod[:, (N_MOD - 1) * D:]).then_inc(s_wm, 16)
                for b in range(B):
                    sp.wait_ge(s_fin, b + 1)
                    sp.dma_start(out[b].rearrange("(t p) d -> p t d", p=P), acc[:, b * T:(b + 1) * T, :])\
                      .then_inc(s_out, 16)
                sp.wait_ge(s_out, 16 * B)

            @block.gpsimd
            def _(pool):
                pool.iota(idx[:], pattern=[[1, E]], base=0, channel_multiplier=0,
                          allow_small_or_imprecise_dtypes=True).then_inc(s_iota, 1)
                pool.memset(acc[:], 0.0).then_inc(s_zero, 1)

                def m_low(b):
                    m = slice(b * S, (b + 1) * S)
                    pool.wait_ge(s_hi, b + 1)
                    pool.tensor_tensor(m_lo[:, m], m_feat[:, m], m_hi[:, m].bitcast(F32), ALU.subtract)\
                        .then_inc(s_lo, 1)

                inverse_root(pool, small, B)
                for b in range(B):
                    m_low(b)
                pool.wait_ge(s_gb, 1)
                shared = [rows3[:, i, :].unsqueeze(1).to_broadcast([P, B, D]) for i in (1, 2)]
                pool.tensor_tensor(gtmp[:, 0], gb[:], shared[0], ALU.mult).then_inc(s_gb2, 1)
                pool.tensor_tensor(gtmp[:, 1], gb[:], shared[1], ALU.mult).then_inc(s_gb2, 1)
                pool.wait_ge(s_gb2, 2)
                for b in range(B):
                    rows = x2_of(b)
                    pool.tensor_tensor(rows, rows, over_tiles(gtmp[:, 1, b, :], T), ALU.add)\
                        .then_inc(s_gb2, 1)
                for b in range(B):
                    inverse_root(pool, small, B + b + 1)

            @block.scalar
            def _(act):
                for b in range(B):
                    m = slice(b * S, (b + 1) * S)
                    act.wait_ge(s_tr, b + 1)
                    act.activation(m_feat[:, m], bank[6 + b % 2][:], ACT.Identity,
                                   bias=cols[:, 0, b:b + 1], scale=cols[:, 1, b:b + 1]).then_inc(s_fe, 1)
                    act.wait_ge(s_fe, b + 1)
                    act.activation(m_hi[:, m], m_feat[:, m], ACT.Copy).then_inc(s_hi, 1)
                    if b == 0:
                        act.wait_ge(s_w1, 16)
                        act.activation(w1_hi[0][:], w1_raw[:, 0, :], ACT.Copy).then_inc(s_whi, 1)
                act.wait_ge(s_small, 16 * N_SMALL)

                up_turns = Turns(act, s_u)
                act.sem_inc(s_g, 1)

                def gelus(e, g):
                    for f in range(FB):
                        up_turns.wait()
                        act.activation(inner[:, g % 2, f, :], bank[f][:], ACT.Gelu,
                                       bias=b1_all[:, e, f:f + 1]).then_inc(s_g, 1)

                def pair(e0, last):
                    for k in range(2):
                        if k == 0 or not last:
                            act.activation(w1_hi[1 - k][:], w1_raw[:, e0 + k + 1, :], ACT.Copy)\
                                .then_inc(s_whi, 1)
                        for g in range(B):
                            gelus(e0 + k, g)

                act.wait_ge(s_lg, 1)
                act.activation(pr[:], logit[:], ACT.Exp).then_inc(s_e, 1)
                with act.Fori(0, LAST // 2) as i:
                    pair(i * 2, False)
                act.wait_ge(s_gatec, 2 * B)
                act.activation(gsh[:], gsh[:], ACT.Gelu).then_inc(s_gelu, 1)
                pair(LAST, True)

            @block.vector
            def _(dve):
                ch, stats = Chain(dve, s_ch), Counted(dve, small[4], T, (B - 1) * T)
                rows = h_tok[:, (B - 1) * T:B * T, :]
                dve.wait_ge(s_xin[B - 1], 16)
                dve.tensor_tensor(x2_of(B - 1), x2_of(B - 1), rows, ALU.add).then_inc(s_x2, 1)
                dve.wait_ge(s_x2, 1)
                layer_norm_moments(dve, ch, stats, x2_of(B - 1), small)
                layer_norm_scale(dve, ch, x2_of(B - 1), small, B, rows, s_h)

                def gate_out(b):
                    dve.wait_ge(s_gate, b + 1)
                    for i in range(2):
                        t = b * T + 2 * i
                        both = bank[4 + i][:, 0:2 * (D + E)].rearrange("p (t n) -> p t n", t=2)
                        ch.step(dve.tensor_copy(logit[:, t:t + 2, :], both[:, :, D:]))
                        dve.tensor_tensor(gsh[:, t:t + 2, :], both[:, :, 0:D],
                                          over_tiles(rows3[:, 0, :], 2), ALU.add).then_inc(s_gatec, 1)

                dve.wait_ge(s_small, 16 * N_SMALL)
                gate_out(0)
                dve.wait_ge(s_whi, 1)
                dve.tensor_tensor(w1_lo[0][:], w1_raw[:, 0, :], w1_hi[0][:].bitcast(F32), ALU.subtract)\
                    .then_inc(s_wlo, 1)
                for b in range(1, B):
                    gate_out(b)

                def wide(a):
                    return a.unsqueeze(2).to_broadcast([P, N, E])

                idxs = idx[:].unsqueeze(1).to_broadcast([P, N, E])
                ch.wait()
                ch.link(dve.tensor_reduce(top[:, 0, :], logit[:], AX.X, ALU.max))
                dve.tensor_tensor(logit[:], logit[:], wide(top[:, 0, :]), ALU.subtract).then_inc(s_lg, 1)
                dve.wait_ge(s_e, 1)
                ch.link(dve.tensor_reduce(top[:, 2, :], pr[:], AX.X, ALU.add))
                ch.link(dve.reciprocal(top[:, 2, :], top[:, 2, :]))
                ch.link(dve.tensor_tensor(pr[:], pr[:], wide(top[:, 2, :]), ALU.mult))
                dve.wait_ge(s_iota, 1)
                for k in range(2):
                    ch.link(dve.tensor_reduce(top[:, k, :], pr[:], AX.X, ALU.max))
                    ch.link(dve.tensor_tensor(eq[:], pr[:], wide(top[:, k, :]), ALU.is_equal))
                    ch.link(dve.tensor_scalar(eq[:], eq[:], -float(E), float(E), ALU.mult, ALU.add))
                    ch.link(dve.tensor_tensor(eq[:], eq[:], idxs, ALU.add))
                    ch.link(dve.tensor_reduce(first[:], eq[:], AX.X, ALU.min))
                    ch.link(dve.tensor_tensor(one[:, k], idxs, wide(first[:]), ALU.is_equal))
                    if k == 0:
                        ch.link(dve.scalar_tensor_tensor(out=pr[:], in0=one[:, 0], scalar=-2.0, in1=pr[:],
                                                         op0=ALU.mult, op1=ALU.add))
                ch.link(dve.tensor_tensor(top[:, 2, :], top[:, 0, :], top[:, 1, :], ALU.add))
                ch.link(dve.reciprocal(top[:, 2, :], top[:, 2, :]))
                for k in range(2):
                    ch.link(dve.tensor_tensor(top[:, k, :], top[:, k, :], top[:, 2, :], ALU.mult))
                    ch.link(dve.tensor_tensor(one[:, k], one[:, k], wide(top[:, k, :]), ALU.mult))
                dve.tensor_tensor(comb[:], one[:, 0], one[:, 1], ALU.add).then_inc(s_cb, 1)
                dve.wait_ge(s_cb, 1)
                dve.wait_ge(s_mod, 1)
                guard(dve, ch, bank[6][:], *(t.rearrange("p b d -> p (b d)")
                                             for t in (gtmp[:, 0], gtmp[:, 1], gb[:]))).then_inc(s_gb, 1)
                dve.wait_ge(s_zero, 1)
                dve.sem_inc(s_a, AHEAD)

                def sums(e, g):
                    dve.wait_ge(s_y, e * B + g + 2)
                    for t in range(T):
                        n = g * T + t
                        if n == 0:
                            dve.wait_ge(s_a, e * N + AHEAD)
                        dve.scalar_tensor_tensor(
                            out=acc[:, n, :], in0=bank[4 + g % 2][:, t * P:(t + 1) * P],
                            scalar=comb[:, n, bass.ds(e, 1)], in1=acc[:, n, :],
                            op0=ALU.mult, op1=ALU.add).then_inc(s_a, 1)

                def base(g):
                    r = slice(g * T, (g + 1) * T)
                    dve.wait_ge(s_b2, g + 1)
                    ch.link(dve.scalar_tensor_tensor(out=gsh[:, r, :], in0=gsh[:, r, :], scalar=0.5,
                                                     in1=bank[6 + g % 2][:].rearrange("p (t d) -> p t d", t=T),
                                                     op0=ALU.mult, op1=ALU.add))
                    dve.wait_ge(s_a, LAST * N + (g + 1) * T + AHEAD)
                    dve.tensor_tensor(acc[:, r, :], acc[:, r, :], gsh[:, r, :], ALU.add).then_inc(s_base, 1)

                def pair(e0, last):
                    for k in range(2):
                        if last and k == 1:
                            dve.wait_ge(s_base, B)
                        if k == 0 or not last:
                            dve.wait_ge(s_whi, e0 + k + 2)
                            dve.tensor_tensor(w1_lo[1 - k][:], w1_raw[:, e0 + k + 1, :],
                                              w1_hi[1 - k][:].bitcast(F32), ALU.subtract).then_inc(s_wlo, 1)
                        for g in range(B):
                            if last and k == 0:
                                dve.wait_ge(s_ct, g + 1)
                                dve.tensor_copy(comb_t[:, g * T:(g + 1) * T, :],
                                                bank[6 + g % 2][0:E, :].rearrange("e (t p) -> e t p", t=T))\
                                    .then_inc(s_ctc, 1)
                            sums(e0 + k, g)
                            if last and k == 0:
                                base(g)
                            if last and k == 1:
                                r = slice(g * T, (g + 1) * T)
                                rows = acc[:, r, :]
                                dve.wait_ge(s_a, (e0 + 1) * N + (g + 1) * T + AHEAD)
                                layer_norm_moments(dve, ch, stats, rows, small)
                                layer_norm_scale(dve, ch, rows, small, B + g + 1, rows)
                                ch.wait()
                                dve.wait_ge(s_gb2, 2 + B)
                                ch.link(dve.tensor_tensor(rows, rows, over_tiles(gtmp[:, 0, g, :], T),
                                                          ALU.mult))
                                dve.tensor_tensor(rows, rows, x2_of(g), ALU.add).then_inc(s_fin, 1)

                with dve.Fori(0, LAST // 2) as i:
                    pair(i * 2, False)
                dve.wait_ge(s_gelu, 1)
                pair(LAST, True)

            @block.tensor
            def _(pe):
                def turn(b):
                    if b == B - 1:
                        pe.wait_ge(s_h, T)
                    if b >= 2:
                        pe.wait_ge(s_fe, b - 1)
                    for t in range(T):
                        mm = pe.transpose(bank[6 + b % 2][:, t * P:(t + 1) * P], h_tok[:, b * T + t, :], ident[:])
                    mm.then_inc(s_tr, 1)

                def gate(b):
                    pe.wait_ge(s_fe, b + 1)
                    if b == 0:
                        pe.wait_ge(s_small, 16 * N_SMALL)
                    else:
                        pe.wait_ge(s_gatec, 2 * b)
                    for t in range(T):
                        i = t % 2 * (D + E)
                        mm = pe.matmul(bank[4 + t // 2][:, i:i + D + E],
                                       m_feat[:, b * S + t * P:b * S + (t + 1) * P], wsg,
                                       start=True, stop=True)
                    mm.then_inc(s_gate, 1)

                def up(e, k, g, first=False):
                    for f in range(FB):
                        n = g * FB + f
                        if not first:
                            pe.wait_ge(s_g, e * B * FB + n - 2)
                        w = slice(f * P, (f + 1) * P)
                        m = slice(g * S, (g + 1) * S)
                        pe.matmul(bank[f][:], w1_hi[k][:, w], m_hi[:, m], start=True, stop=False)
                        pe.matmul(bank[f][:], w1_hi[k][:, w], m_lo[:, m], start=False, stop=False)
                        pe.matmul(bank[f][:], w1_lo[k][:, w], m_hi[:, m], start=False, stop=True)\
                            .then_inc(s_u, 1)

                def down(e, g):
                    pe.wait_ge(s_g, e * B * FB + (g + 1) * FB + 1)
                    pe.wait_ge(s_a, e * N + (g - 1) * T + AHEAD)
                    for t in range(T):
                        for f in range(FB):
                            mm = pe.matmul(bank[4 + g % 2][:, t * P:(t + 1) * P],
                                           inner[:, g % 2, f, t * P:(t + 1) * P],
                                           w2_all[:, e, f, :], start=(f == 0), stop=(f == FB - 1))
                    mm.then_inc(s_y, 1)

                def turn_weights(g):
                    if g >= 2:
                        pe.wait_ge(s_base, g - 1)
                    for t in range(T):
                        mm = pe.transpose(bank[6 + g % 2][0:E, t * P:(t + 1) * P], comb[:, g * T + t, :],
                                          ident[:])
                    mm.then_inc(s_ct, 1)

                def chosen_b2(g):
                    pe.wait_ge(s_ctc, g + 1)
                    for t in range(T):
                        mm = pe.matmul(bank[6 + g % 2][:, t * P:(t + 1) * P], comb_t[:, g * T + t, :],
                                       b2_all, start=True, stop=True)
                    mm.then_inc(s_b2, 1)

                def pair(e0, last):
                    for k in range(2):
                        for g in range(B):
                            if last and k == 0:
                                turn_weights(g)
                            if g + 1 < B:
                                up(e0 + k, k, g + 1)
                            elif k == 0 or not last:
                                pe.wait_ge(s_wlo, e0 + k + 2)
                                up(e0 + k + 1, 1 - k, 0)
                            if last and k == 0:
                                chosen_b2(g)
                            down(e0 + k, g)

                turn(0)
                turn(1)
                gate(0)
                turn(2)
                gate(1)
                turn(3)
                gate(2)
                gate(3)
                pe.wait_ge(s_lo, 1)
                pe.wait_ge(s_wlo, 1)
                up(0, 0, 0, first=True)
                pe.wait_ge(s_lo, B)
                pe.wait_ge(s_gatec, 2 * B)
                pe.wait_ge(s_w2, 16 * FB)
                pe.wait_ge(s_wm, 16)
                for b in range(B):
                    mm = pe.matmul(bank[6][:, b * D:(b + 1) * D], silu_c[:, b:b + 1].to_broadcast([P, P]),
                                   wm[:], start=True, stop=True)
                mm.then_inc(s_mod, 1)
                pe.sem_inc(s_y, 1)
                with pe.Fori(0, LAST // 2) as i:
                    pair(i * 2, False)
                pe.wait_ge(s_cb, 1)
                pe.wait_ge(s_gb, 1)
                pair(LAST, True)


_INS = ['L0_attn_x', 'L0_attn_W_qkv', 'L0_attn_W_r', 'L0_attn_W_o', 'L0_attn_u', 'L0_attn_v',
        'L0_attn_ln1_g', 'L0_attn_ln1_b', 'L0_attn_W_ff1', 'L0_attn_b_ff1', 'L0_attn_W_ff2',
        'L0_attn_b_ff2', 'L0_attn_ln2_g', 'L0_attn_ln2_b', 'L0_ffn_W1', 'L0_ffn_b1', 'L0_ffn_W2',
        'L0_ffn_b2', 'L0_ffn_gate_W', 'L0_ffn_shared_W', 'L0_ffn_shared_b', 'L0_ffn_gamma',
        'L0_ffn_beta', 'L0_c', 'L0_wmod']


def kernel(**inputs):
    import numpy as _np
    import concourse.bacc as _bacc
    from concourse import mybir as _mybir
    from concourse.bass_utils import run_bass_kernel_spmd as _run

    nc = _bacc.Bacc("TRN2", target_bir_lowering=False, num_devices=1)
    arrays, args = {}, []
    for name in _INS:
        a = _np.ascontiguousarray(inputs[name])
        arrays[f"in_{name}"] = a
        args.append(nc.dram_tensor(f"in_{name}", a.shape, _mybir.dt.from_np(a.dtype),
                                   kind="ExternalInput").ap())
    at = _np.arange(S - 1, -1, -1, dtype=_np.float32)
    freq = (_np.float32(1.0) / _np.float32(10000.0)
            ** (_np.arange(0, D, 2, dtype=_np.float32) / _np.float32(D))).astype(_np.float32)
    ang = freq[:, None] * at[None, :]
    arrays["pos_t"] = _np.concatenate([_np.sin(ang), _np.cos(ang)], axis=0).astype(_np.float32)
    args.append(nc.dram_tensor("pos_t", (D, S), _mybir.dt.float32, kind="ExternalInput").ap())
    args.append(nc.dram_tensor("out_0", (B, S, D), _mybir.dt.float32, kind="ExternalOutput").ap())
    build(nc, *args)
    r = _run(nc, [arrays], core_ids=[0])
    return r.results[0]["out_0"]
```
